# Optimizing a Trainium2 kernel written in Bass

```python
import numpy as np
import jax
import jax.numpy as jnp

def _softmax(x, axis=-1):
    return jax.nn.softmax(x, axis=axis)
def _gelu(x):
    return jax.nn.gelu(x, approximate=True)
def _silu(x):
    return jax.nn.silu(x)
def _sigmoid(x):
    return jax.nn.sigmoid(x)
def _layernorm(x, axis=-1, eps=1e-5):
    m = jnp.mean(x, axis=axis, keepdims=True)
    v = jnp.var(x, axis=axis, keepdims=True)
    return (x - m) / jnp.sqrt(v + eps)
def _scatter_add(tgt, idx, src, axis=0):
    return tgt.at[idx].add(src)
def _segment_sum(src, seg, n):
    return jax.ops.segment_sum(src, seg, n)

kernel_name = 'mk_conv_preact_d2_conv_nchw32_59389a'

def setup_inputs(seed: int = 0):
    np.random.seed(seed)
    _w = jnp.asarray
    def _rec_inputs():
        import jax
        import jax.numpy as jnp
        _gk = jax.random.key(seed)
        x = -7.109e-05 + 0.9999 * jax.random.normal(jax.random.fold_in(_gk, 1), (8, 32, 512, 512), jnp.float32)
        return x
    x = _rec_inputs()
    def _L0_conv_setup():
        import jax, jax.numpy as jnp
        import numpy as np
        R = 5
        ALPHA = 0.65
        NEG = -1e+30

        def _harmonic_basis(theta, K):
            feats = []
            for k in range(1, K + 1):
                m = (k + 1) // 2
                feats.append(jnp.cos(m * theta) if k % 2 == 1 else jnp.sin(m * theta))
            return jnp.stack(feats, axis=-1)

        def morphological_kernel(finsler_params, r, alpha):
            coords = jnp.arange(-r, r + 1, dtype=jnp.float32)
            yy, xx = jnp.meshgrid(coords, coords, indexing='ij')
            rho = jnp.sqrt(xx * xx + yy * yy)
            theta = jnp.arctan2(yy, xx)
            K = finsler_params.shape[-1]
            B = _harmonic_basis(theta, K)
            g = jnp.einsum('ck,ijk->cij', finsler_params, B)
            e = 2.0 * alpha / (2.0 * alpha - 1.0)
            nu = (2.0 * alpha - 1.0) * (2.0 * alpha) ** (-e)
            return nu * (rho ** e)[None, :, :] * jnp.exp(-e * g)

        def dilation(u, kernel, r):
            Bn, C, H, W = u.shape
            ks = 2 * r + 1
            pad = jnp.pad(u, ((0, 0), (0, 0), (r, r), (r, r)), constant_values=NEG)
            kflat = kernel.reshape(C, ks * ks)

            def body(acc, idx):
                di = idx // ks
                dj = idx % ks
                sl = jax.lax.dynamic_slice(pad, (0, 0, di, dj), (Bn, C, H, W))
                acc = jnp.maximum(acc, sl - kflat[:, idx][None, :, None, None])
                return (acc, None)
            acc0 = jnp.full((Bn, C, H, W), NEG, dtype=u.dtype)
            acc, _ = jax.lax.scan(body, acc0, jnp.arange(ks * ks))
            return acc
        key = jax.random.key(seed)
        k1, k2 = jax.random.split(key)
        inp = jax.random.normal(k1, (8, 32, 512, 512), dtype=jnp.float32)
        fp = jax.random.uniform(k2, (32, 6), dtype=jnp.float32, minval=-0.5, maxval=0.5)
        return {'input': inp, 'finsler_params': fp}
    _L0_conv_all = _L0_conv_setup()
    _L0_conv_in = {k: v for k, v in _L0_conv_all.items() if k in ('finsler_params', )}
    del _L0_conv_all

    def _L1_conv_setup():
        import jax, jax.numpy as jnp
        import numpy as np

        def conv1x1(x, w, b):
            return jnp.einsum('bchw,oc->bohw', x, w) + b[None, :, None, None]
        key = jax.random.key(seed)
        ks = jax.random.split(key, 11)
        B, C, H, W = (8, 32, 512, 512)
        x = jax.random.normal(ks[0], (B, C, H, W), dtype=jnp.float32)
        s32 = 1.0 / np.sqrt(32.0)
        s64 = 1.0 / np.sqrt(64.0)
        return {'x': x, 'w_ck': jax.random.normal(ks[1], (1, 32), dtype=jnp.float32) * s32, 'b_ck': jax.random.normal(ks[2], (1,), dtype=jnp.float32) * s32, 'w_cq': jax.random.normal(ks[3], (32, 32), dtype=jnp.float32) * s32, 'b_cq': jax.random.normal(ks[4], (32,), dtype=jnp.float32) * s32, 'w_sk': jax.random.normal(ks[5], (32, 32), dtype=jnp.float32) * s32, 'b_sk': jax.random.normal(ks[6], (32,), dtype=jnp.float32) * s32, 'w_sq': jax.random.normal(ks[7], (32, 32), dtype=jnp.float32) * s32, 'b_sq': jax.random.normal(ks[8], (32,), dtype=jnp.float32) * s32, 'w_f': jax.random.normal(ks[9], (32, 64), dtype=jnp.float32) * s64, 'b_f': jax.random.normal(ks[10], (32,), dtype=jnp.float32) * s64}
    _L1_conv_all = _L1_conv_setup()
    _L1_conv_in = {k: v for k, v in _L1_conv_all.items() if k in ('w_ck', 'b_ck', 'w_cq', 'b_cq', 'w_sk', 'b_sk', 'w_sq', 'b_sq', 'w_f', 'b_f', )}
    del _L1_conv_all

    return {
        "x": x,
        "L0_conv_finsler_params": _L0_conv_in["finsler_params"],
        "L1_conv_w_ck": _L1_conv_in["w_ck"],
        "L1_conv_b_ck": _L1_conv_in["b_ck"],
        "L1_conv_w_cq": _L1_conv_in["w_cq"],
        "L1_conv_b_cq": _L1_conv_in["b_cq"],
        "L1_conv_w_sk": _L1_conv_in["w_sk"],
        "L1_conv_b_sk": _L1_conv_in["b_sk"],
        "L1_conv_w_sq": _L1_conv_in["w_sq"],
        "L1_conv_b_sq": _L1_conv_in["b_sq"],
        "L1_conv_w_f": _L1_conv_in["w_f"],
        "L1_conv_b_f": _L1_conv_in["b_f"],
    }

def reference(x, L0_conv_finsler_params, L1_conv_w_ck, L1_conv_b_ck, L1_conv_w_cq, L1_conv_b_cq, L1_conv_w_sk, L1_conv_b_sk, L1_conv_w_sq, L1_conv_b_sq, L1_conv_w_f, L1_conv_b_f):
    import jax
    import jax.numpy as jnp
    def _L0_conv_ref(input, finsler_params):
        import jax, jax.numpy as jnp
        import numpy as np
        R = 5
        ALPHA = 0.65
        NEG = -1e+30

        def _harmonic_basis(theta, K):
            feats = []
            for k in range(1, K + 1):
                m = (k + 1) // 2
                feats.append(jnp.cos(m * theta) if k % 2 == 1 else jnp.sin(m * theta))
            return jnp.stack(feats, axis=-1)

        def morphological_kernel(finsler_params, r, alpha):
            coords = jnp.arange(-r, r + 1, dtype=jnp.float32)
            yy, xx = jnp.meshgrid(coords, coords, indexing='ij')
            rho = jnp.sqrt(xx * xx + yy * yy)
            theta = jnp.arctan2(yy, xx)
            K = finsler_params.shape[-1]
            B = _harmonic_basis(theta, K)
            g = jnp.einsum('ck,ijk->cij', finsler_params, B)
            e = 2.0 * alpha / (2.0 * alpha - 1.0)
            nu = (2.0 * alpha - 1.0) * (2.0 * alpha) ** (-e)
            return nu * (rho ** e)[None, :, :] * jnp.exp(-e * g)

        def dilation(u, kernel, r):
            Bn, C, H, W = u.shape
            ks = 2 * r + 1
            pad = jnp.pad(u, ((0, 0), (0, 0), (r, r), (r, r)), constant_values=NEG)
            kflat = kernel.reshape(C, ks * ks)

            def body(acc, idx):
                di = idx // ks
                dj = idx % ks
                sl = jax.lax.dynamic_slice(pad, (0, 0, di, dj), (Bn, C, H, W))
                acc = jnp.maximum(acc, sl - kflat[:, idx][None, :, None, None])
                return (acc, None)
            acc0 = jnp.full((Bn, C, H, W), NEG, dtype=u.dtype)
            acc, _ = jax.lax.scan(body, acc0, jnp.arange(ks * ks))
            return acc
        kernel = morphological_kernel(finsler_params, R, ALPHA)
        return dilation(input, kernel, R)

    def _L1_conv_ref(x, w_ck, b_ck, w_cq, b_cq, w_sk, b_sk, w_sq, b_sq, w_f, b_f):
        import jax, jax.numpy as jnp
        import numpy as np

        def conv1x1(x, w, b):
            return jnp.einsum('bchw,oc->bohw', x, w) + b[None, :, None, None]
        B, C, H, W = x.shape
        HW = H * W
        chn_key = conv1x1(x, w_ck, b_ck)
        chn_query = conv1x1(x, w_cq, b_cq)
        q = chn_query.reshape(B, C, HW)
        k = chn_key.reshape(B, HW)
        chn_rel = jnp.einsum('bcn,bn->bc', q, k)
        chn_gate = 1.0 - jax.nn.sigmoid(chn_rel)
        chn_value = chn_gate[:, :, None, None] * x
        spa_key = conv1x1(x, w_sk, b_sk)
        spa_query = conv1x1(x, w_sq, b_sq)
        sq_u = spa_query.reshape(B, HW, C)
        sk_u = spa_key.reshape(B, HW, C).mean(axis=1)
        spa_rel = jnp.einsum('bnc,bc->bn', sq_u, sk_u)
        spa_gate = 1.0 - jax.nn.sigmoid(spa_rel)
        spa_value = spa_gate.reshape(B, 1, H, W) * x
        cat = jnp.concatenate([chn_value, spa_value], axis=1)
        return conv1x1(cat, w_f, b_f)

    def _gn(v, G=16, eps=1e-5):
        B_, C_, H_, W_ = v.shape
        g = v.reshape(B_, G, C_ // G, H_, W_)
        m = jnp.mean(g, axis=(2, 3, 4), keepdims=True)
        s = jnp.var(g, axis=(2, 3, 4), keepdims=True)
        return ((g - m) / jnp.sqrt(s + eps)).reshape(v.shape)

    def _ln_c(v, eps=1e-6):
        m = jnp.mean(v, axis=1, keepdims=True)
        s = jnp.var(v, axis=1, keepdims=True)
        return (v - m) / jnp.sqrt(s + eps)

    def _ln_t(v, eps=1e-5):
        m = jnp.mean(v, axis=-1, keepdims=True)
        s = jnp.var(v, axis=-1, keepdims=True)
        return (v - m) / jnp.sqrt(s + eps)

    def _to_tokens(v):
        B_, C_, H_, W_ = v.shape
        return v.reshape(B_, C_, H_ * W_).transpose(0, 2, 1)
    def _from_tokens(t, like):
        B_, C_, H_, W_ = like.shape
        return t.transpose(0, 2, 1).reshape(B_, C_, H_, W_)

    x = x + _L0_conv_ref(_gn(x), L0_conv_finsler_params)
    x = x + _L1_conv_ref(_gn(x), L1_conv_w_ck, L1_conv_b_ck, L1_conv_w_cq, L1_conv_b_cq, L1_conv_w_sk, L1_conv_b_sk, L1_conv_w_sq, L1_conv_b_sq, L1_conv_w_f, L1_conv_b_f)
    return x


_drawn_inputs = setup_inputs


def setup_inputs(seed=0):
    import zlib

    import numpy as np

    out = dict(_drawn_inputs(seed))
    spreads = {}
    factors = {'L1_conv_w_sk': 8.0, 'L1_conv_b_sk': 8.0, 'L1_conv_w_sq': 8.0, 'L1_conv_b_sq': 8.0}
    for name, (base, spread) in spreads.items():
        noise = np.random.default_rng([zlib.crc32(name.encode()), seed]).standard_normal(out[name].shape)
        drawn = base * np.exp(spread * noise) if base else spread * noise
        out[name] = jnp.asarray(drawn.astype(out[name].dtype))
    for name, factor in factors.items():
        out[name] = (out[name] * factor).astype(out[name].dtype)
    return out
```

```python
from contextlib import ExitStack

import numpy as np

import concourse.bass as bass
from concourse import mybir

ALU = mybir.AluOpType
ACT = mybir.ActivationFunctionType
F32 = mybir.dt.float32
BF16 = mybir.dt.bfloat16
I32 = mybir.dt.int32
AX_X = mybir.AxisListType.X
RMAX = bass.bass_isa.ReduceOp.max

B, C, H, W = 8, 32, 512, 512
HW = H * W
P = 128
PAIRS = B // 2
R = 5
KS = 2 * R + 1
TAPS = KS * KS - 1
QUARTERS = 4
BANDS = P // (2 * QUARTERS)
TR, TC = H // BANDS, W // QUARTERS
HR, HC = TR + 2 * R, TC + 2 * R
BLK = TR * TC
XLEN = HR * HC + 12
CENTRE = R * HC + R
GC = 16
EPS = 1e-5
NEG = -1e30
ALPHA = 0.65
E_EXP = 2.0 * ALPHA / (2.0 * ALPHA - 1.0)
NU = (2.0 * ALPHA - 1.0) * (2.0 * ALPHA) ** (-E_EXP)
FIRST = 8
FIXED = 12
COUNT_AT = 9
GRP = 9
NEAR = 5
GROUPS = (TAPS - FIXED) // GRP
BETA = 8.0
OFFS = 24.0
KCAP = 16.5
AT = 4096
CH = 1024
NCH = AT // CH
LOADS = 16 * 4 * QUARTERS
STORES = 16 * 2 * QUARTERS
BW = 32
MT = AT // BW
QB = TAPS // QUARTERS

CONSTS = 2 + 5 * 4 + 2 * 4 + 3 * 4 + 2

_W = dict(ident=P, same=P, qfold=P, bd=P, img=2, fold=32, sel=8 * P, iota=TAPS, radial=TAPS, offq=QB)
CO, _at = {}, 0
for _k, _n in _W.items():
    CO[_k] = (_at, _at + _n)
    _at += _n
NCONST = _at


def shape_constants():
    p = np.arange(P)
    c = np.zeros((P, NCONST), np.float32)

    def put(name, a):
        c[:, CO[name][0]:CO[name][1]] = a

    put("ident", p[:, None] == p[None, :])
    put("same", p[:, None] % 2 == p[None, :] % 2)
    put("qfold", p[:, None] % 32 == p[None, :] % 32)
    put("bd", p[:, None] // 32 == p[None, :] // 32)
    put("img", p[:, None] % 2 == np.arange(2)[None, :])
    put("fold", p[:, None] % 32 == np.arange(32)[None, :])
    k = np.arange(8)
    put("sel", ((p[:, None, None] % 32) == (p[None, None, :] // 32) * 8 + k[None, :, None]).reshape(P, -1))
    put("iota", np.arange(TAPS)[None, :])
    d = np.arange(-R, R + 1)
    yy, xx = (a.reshape(-1) for a in np.meshgrid(d, d, indexing="ij"))
    keep = (yy != 0) | (xx != 0)
    yy, xx = yy[keep], xx[keep]
    rho, theta = np.sqrt(yy * yy + xx * xx), np.arctan2(yy, xx)
    put("radial", (NU * rho ** E_EXP)[None, :])
    off = (yy + R) * HC + xx + R
    put("offq", off.reshape(QUARTERS, QB)[p // 32])
    basis = np.stack([np.cos((m + 1) // 2 * theta) if m % 2 else np.sin((m + 1) // 2 * theta)
                      for m in range(1, 7)]).astype(np.float32)
    t = (p // 32)[:, None] * QB + np.arange(QB)[None, :]
    tie = (np.arange(TAPS)[None, None, :] < t[:, :, None]).astype(np.float32).reshape(P, -1)
    return {"cst": c, "basis": basis, "tie": tie}


def build(nc, x, fp, w_ck, b_ck, w_cq, b_cq, w_sk, b_sk, w_sq, b_sq, w_f, b_f, cst_d, basis_d, tie_d, out):
    x1_d = nc.dram_tensor("x1_scratch", [B, C, H, W], F32, kind="Internal").ap()
    ktab_d = nc.dram_tensor("ktab_scratch", [C, 2 * TAPS], F32, kind="Internal").ap()
    otab_d = nc.dram_tensor("otab_scratch", [C, TAPS], I32, kind="Internal").ap()

    with ExitStack() as ctx:
        def sb(name, shape, dt=F32):
            return ctx.enter_context(nc.sbuf_tensor(name, shape, dt))

        def sem(name):
            return ctx.enter_context(nc.semaphore(name))

        xt = [sb(f"xt{s}", [P, XLEN]) for s in range(2)]
        accf = sb("acc_first", [P, BLK])
        acc = [sb(f"acc{s}", [P, BLK]) for s in range(2)]
        junk = sb("junk", [P, HR // 2 * HC], BF16)
        pst = sb("stat_tile", [P, BLK])
        at = [sb(f"att{s}", [P, AT]) for s in range(2)]
        gxf = sb("gated", [P, 2 * CH])
        gx = gxf[:, :].rearrange("p (s f) -> p s f", s=2)
        gates = sb("gates", [P, HW // BW // QUARTERS])
        wj = sb("w_spatial", [P, BW, P])
        krow = sb("krow", [P, 2, 2 * TAPS])
        orow = sb("orow", [1, 2, TAPS], I32)
        pen = sb("pen", [P, 2, TAPS])
        flag = sb("flag", [P, TAPS])
        cst = sb("cst_sb", [P, NCONST])
        cur = sb("cur", [P, 2, 8])
        diag = sb("diag", [P, 2, P])
        selk = sb("selk", [P, 2, P])
        ex = sb("ex", [P, 2, 4])
        bnd = sb("bnd", [P, 4])
        cntp = sb("cntp", [P, 2])
        cntm = sb("cntm", [P, 1])
        cnt = sb("cnt", [1, 2], I32)
        pacc = sb("pacc", [P, 2, 3])
        xacc = sb("xacc", [P, 2, 8])
        yacc = sb("yacc", [P, 2, 8])
        stat = sb("stat", [P, C, 8])
        px = [sb(f"px{i}", [P, C]) for i in range(2)]
        p1 = [sb(f"p1{i}", [P, C]) for i in range(2)]
        csum = sb("csum", [P, C, 2])
        atab = sb("atab", [P, 8, 8])
        tb = sb("tb", [P, 4, C])
        tb4 = sb("tb4", [P, 4, QUARTERS, C])
        cols = sb("cols", [P, 4, 2])
        st = sb("st", [P, 8, C])
        wf = sb("weights", [P, 9, P])
        wsq, wcq, wf1, wf2, wck, wckp, ipw, wtmp = (wf[:, i, :] for i in range(8))
        wv, wa, wb = (sb(n, [P, P]) for n in ("wv", "wa", "wb"))
        bcol = sb("bcol", [P, 5])
        ones = sb("ones", [P, P])
        carved = 0

        def carve(rows, n):
            nonlocal carved
            carved += n
            return gxf[0:rows, carved - n:carved]

        wraw = carve(32, 5 * P).rearrange("p (i m) -> p i m", i=5)
        wckr, fpt, basis = carve(1, P), carve(6, P), carve(6, TAPS)
        kk, kq, rank, sums = (carve(P, n) for n in (TAPS, QB, QB, 2 * TAPS))
        krow_o, orow_o = carve(32, 2 * TAPS), carve(32, TAPS).bitcast(I32)
        col = sb("col", [P, 24])
        skb = sb("skb", [P, BW])
        skr = sb("skr", [P, BW])
        classes = sb("classes", [32, 2, BW])
        pp = sb("pp", [32, BW])
        (W_SUM, W_NORM, W_INV, W_ALPHA, W_IALPHA, W_IDEN, WS_SUM, RM, BIASV, BIASZ, SKSUM, ASUM, ZC, KP, UC,
         REL, GATE, RG, R5, BIASO, TMP, WCOL, WRC, C_EK) = range(24)

        def cc(i):
            return col[:, i:i + 1]

        def const(name):
            return cst[:, CO[name][0]:CO[name][1]]

        ident = const("ident")
        sel = const("sel").rearrange("p (k m) -> p k m", k=8)

        ps_mix = ctx.enter_context(nc.psum_tensor("ps_mix", [P, CH], F32))
        ps_y = ctx.enter_context(nc.psum_tensor("ps_y", [P, CH], F32))
        ps_g = ctx.enter_context(nc.psum_tensor("ps_g", [P, CH], F32))
        ps_col = ctx.enter_context(nc.psum_tensor("ps_col", [P, 512], F32))
        ps_t = ctx.enter_context(nc.psum_tensor("ps_t", [P, 512], F32))
        small = ps_t[:, P:512]

        const_in = sem("const_in")
        tie_in = sem("tie_in")
        filled = sem("filled")
        tabs_out = sem("tabs_out")
        x_in = [sem(f"x_in{s}") for s in range(2)]
        row_in = [sem(f"row_in{s}") for s in range(2)]
        x_free = [sem(f"x_free{s}") for s in range(2)]
        cur_free = [sem(f"cur_free{s}") for s in range(2)]
        cur_set = sem("cur_set")
        diag_set = sem("diag_set")
        pen_set = sem("pen_set")
        tap_done = sem("tap_done")
        junk_w = sem("junk_w")
        sums_in = sem("sums_in")
        bnd_step = sem("bnd_step")
        counted = sem("counted")
        cnt_step = sem("cnt_step")
        mix_ready = sem("mix_ready")
        mix_out = sem("mix_out")
        xs_step = sem("xs_step")
        csum_ready = sem("csum_ready")
        csum_out = sem("csum_out")
        acc_free = [sem(f"acc_free{s}") for s in range(2)]
        x1_st = [sem(f"x1_st{s}") for s in range(2)]
        pst_in = sem("pst_in")
        pst_free = sem("pst_free")
        ps_step = sem("ps_step")
        at_in = [sem(f"at_in{s}") for s in range(2)]
        at_free = [sem(f"at_free{s}") for s in range(2)]
        z_ready = sem("z_ready")
        z_out = sem("z_out")
        y_ready = sem("y_ready")
        y_out = sem("y_out")
        a_kept = sem("a_kept")
        g_ready = sem("g_ready")
        gx_ready = sem("gx_ready")
        selk_set = sem("selk_set")
        wj_set = sem("wj_set")
        out_st = [sem(f"out_st{s}") for s in range(2)]
        to_pe = sem("to_pe")
        to_act = sem("to_act")
        to_pool = sem("to_pool")
        pe_small = sem("pe_small")
        act_small = sem("act_small")
        dve_small = sem("dve_small")
        passed = sem("passed")
        tabs_small = sem("tabs_small")

        block = ctx.enter_context(nc.Block())

        def loop(eng, count, body):
            with eng.Fori(0, count // 2) as i:
                for u in range(2):
                    body(i, u)

        def own_wait(eng, semaphore, value):
            eng.wait_ge(semaphore, value)
            eng.sem_inc(passed, 1)


        def schedule():
            for g in range(PAIRS + 1):
                for blk in range(4):
                    yield g, blk

        def halo_loads(eng, g, c, s):
            X = xt[s][:, 0:HR * HC].rearrange("p (r c) -> p r c", c=HC)
            img = x.rearrange("b c h w -> c b h w")
            for q in range(QUARTERS):
                lo = R if q == 0 else 0
                hi = HC - R if q == QUARTERS - 1 else HC
                col0 = q * TC - R + lo
                n = hi - lo
                src = img[bass.ds(c, 1), 2 * g:2 * g + 2, :, :]
                p0 = 32 * q
                eng.dma_start(X[p0:p0 + 2, R:HR, lo:hi],
                              src[0, :, 0:TR + R, col0:col0 + n]).then_inc(x_in[s], 16)
                for m in range(2):
                    base = src[0, m, TR - R:TR - R + HR, col0:col0 + n]
                    mid = bass.AP(base.tensor, base.offset, [[TR * W, BANDS - 2], [W, HR], [1, n]])
                    eng.dma_start(X[p0 + 2 + m:p0 + 30:2, :, lo:hi], mid).then_inc(x_in[s], 16)
                eng.dma_start(X[p0 + 30:p0 + 32, 0:TR + R, lo:hi],
                              src[0, :, H - TR - R:H, col0:col0 + n]).then_inc(x_in[s], 16)

        def stat_load(eng, g, c):
            base = x.rearrange("b c h w -> c b (h w)")[bass.ds(c, 1), 2 * g:2 * g + 2, 0:BLK]
            src = bass.AP(base.tensor, base.offset, [[BLK, HW // BLK], [C * HW, 2], [1, BLK]])
            eng.dma_start(pst[:, :], src).then_inc(pst_in, 16)

        from_one = (tap_done, sums_in, csum_out, csum_ready, xs_step, junk_w, mix_out, y_out, z_out, gx_ready, a_kept,
                    g_ready, x1_st[0], x1_st[1], out_st[0], out_st[1])

        def tile_of(a, b, t):
            base = a[b].rearrange("c h w -> c (h w)")[:, bass.ds(t * AT, AT)]
            return bass.AP(base.tensor, base.offset, [[HW // QUARTERS, QUARTERS], [HW, C], [1, AT]])

        @block.sync
        def _(sp):
            for s in from_one:
                sp.sem_inc(s, 1)
            sp.dma_start(cst[:, :], cst_d).then_inc(const_in, 16)
            sp.dma_start(basis[:, :], basis_d).then_inc(const_in, 16)
            for i, (w, lo) in enumerate(((w_sq, 0), (w_cq, 0), (w_f, 0), (w_f, 32), (w_sk, 0))):
                for q in range(QUARTERS):
                    sp.dma_start(wraw[:, i, 32 * q:32 * q + 32], w[:, lo:lo + 32]).then_inc(const_in, 16)
            with nc.allow_non_contiguous_dma("a few hundred elements, once"):
                for q in range(QUARTERS):
                    sp.dma_start(wckr[:, 32 * q:32 * q + 32], w_ck).then_inc(const_in, 16)
                    sp.dma_start(fpt[:, 32 * q:32 * q + 32], fp.rearrange("c k -> k c")).then_inc(const_in, 16)
                for i, b in enumerate((b_sq, b_cq, b_f)):
                    for q in range(4):
                        sp.dma_start(bcol[32 * q:32 * q + 32, i:i + 1],
                                     b.rearrange("(c a) -> c a", a=1)).then_inc(const_in, 16)
                sp.dma_start(bcol[:, 3:4], bass.AP(b_ck.tensor, b_ck.offset, [[0, P], [1, 1]])).then_inc(const_in, 16)
                sp.dma_start(bcol[0:32, 4:5], b_sk.rearrange("(c a) -> c a", a=1)).then_inc(const_in, 16)
            sp.dma_start(accf[:, 0:QB * TAPS], tie_d).then_inc(tie_in, 16)
            sp.wait_ge(tabs_small, 2)
            sp.dma_start(ktab_d, krow_o[:, :]).then_inc(tabs_out, 16)
            sp.dma_start(otab_d, orow_o[:, :]).then_inc(tabs_out, 16)

            def stat_step(g):
                def body(i2, u):
                    n = g * C + 2 * i2 + u
                    sp.wait_ge(pst_free, n + 1)
                    stat_load(sp, g, 2 * i2 + u)
                return body

            loop(sp, C, stat_step(0))
            sp.wait_ge(tabs_out, 32)
            sp.wait_ge(filled, 4)
            for g, blk in schedule():
                img, phase = divmod(blk, 2)
                if g > 0 and blk == 0:
                    for s in range(2):
                        sp.wait_ge(x1_st[s], STORES * (C // 2) * g + 1)

                def attention_loads(i, u, g=g, blk=blk, img=img, phase=phase):
                    k = 2 * i + u
                    ls = ((g - 1) * 4 + blk) * 8 + k
                    stored = ((g - 1) * 2 + img) * 8 + (k if phase == 1 else 0)
                    for s in range(2):
                        sp.wait_ge(at_free[s], ls + 1)
                        sp.wait_ge(out_st[s], 16 * stored + 1)
                        sp.dma_start(at[s][:, :], tile_of(x1_d, 2 * (g - 1) + img, 2 * k + s)).then_inc(at_in[s], 16)

                def body(i, u, g=g, blk=blk):
                    if g == PAIRS:
                        attention_loads(i, u)
                        return
                    i2 = 4 * blk + i
                    c = 2 * i2 + u
                    sp.wait_ge(x_free[u], g * (C // 2) + i2 + 1)
                    krs = bass.AP(ktab_d.tensor, 0, [[2 * TAPS, C], [1, 2 * TAPS]])[bass.ds(c, 1), :]
                    sp.dma_start(krow[:, u, :], bass.AP(krs.tensor, krs.offset, [[0, P], [1, 2 * TAPS]])
                                 ).then_inc(row_in[u], 16)
                    sp.dma_start(orow[:, u, :], otab_d[bass.ds(c, 1), :]).then_inc(row_in[u], 16)
                    halo_loads(sp, g, c, u)
                    if g > 0:
                        attention_loads(i, u)
                    if g + 1 < PAIRS:
                        stat_step(g + 1)(i2, u)
                loop(sp, 8, body)

        @block.gpsimd
        def _(pool):
            pool.memset(ones[:, :], 1.0).then_inc(filled, 1)
            pool.memset(xt[0][:, :], NEG).then_inc(filled, 1)
            pool.memset(xt[1][:, :], NEG).then_inc(filled, 1)
            pool.memset(cc(C_EK), -2.0 * OFFS).then_inc(filled, 1)

            to_pool_n = 0
            for g, blk in schedule():
                img, phase = divmod(blk, 2)
                if blk == 0 and g < PAIRS:
                    to_pool_n += 1
                    pool.wait_ge(to_pool, to_pool_n)
                if g > 0 and phase == 0:
                    to_pool_n += 1
                    pool.wait_ge(to_pool, to_pool_n)
                    pool.tensor_tensor(wj[:, :, :], wsq.unsqueeze(1).to_broadcast([P, BW, P]),
                                       skr[:, :].unsqueeze(2).to_broadcast([P, BW, P]), ALU.mult).then_inc(wj_set, 1)

                def body(i, u, g=g, blk=blk, img=img, phase=phase):
                    i2 = 4 * blk + i
                    n = g * C + 2 * i2 + u
                    c = 2 * i2 + u
                    if g < PAIRS:
                        own_wait(pool, cur_free[u], g * (C // 2) + i2 + 1)
                        pool.tensor_copy(cur[:, u, :], stat[:, bass.ds(c, 1), :].rearrange("p a k -> p (a k)")
                                         ).then_inc(cur_set, 1)
                        own_wait(pool, cur_set, n + 1)
                        pool.tensor_scalar(diag[:, u, :], ident, cur[:, u, 1:2], None, ALU.mult).then_inc(diag_set, 1)
                    if g > 0:
                        k = 2 * i + u
                        ls = ((g - 1) * 4 + blk) * 8 + k
                        b = 2 * (g - 1) + img
                        if phase == 1:
                            kb = ((g - 1) * 2 + img) * 8 + k
                            own_wait(pool, g_ready, 8 * kb + 1)
                            pool.tensor_copy(selk[:, u, :], sel[:, bass.ds(k, 1), :].rearrange("p a m -> p (a m)")
                                             ).then_inc(selk_set, 1)
                    if g < PAIRS:
                        own_wait(pool, sums_in, n + 1 + 1)
                        pool.tensor_tensor(bnd[:, 0:2], ex[:, u, 0:4:2], ex[:, u, 1:4:2], ALU.add).then_inc(bnd_step, 1)
                        own_wait(pool, bnd_step, 4 * n + 1)
                        pool.tensor_scalar(bnd[:, 2:4], bnd[:, 0:2], 1e-37, 1.01, ALU.add, ALU.mult
                                           ).then_inc(bnd_step, 2)
                        own_wait(pool, bnd_step, 4 * n + 3)
                        pool.tensor_tensor(bnd[:, 0:1], bnd[:, 2:3], bnd[:, 3:4], ALU.mult).then_inc(bnd_step, 1)
                        own_wait(pool, counted, n + 1)
                        pool.partition_all_reduce(cntm[:, :], cntp[:, u:u + 1], P, RMAX).then_inc(cnt_step, 1)
                        own_wait(pool, cnt_step, 2 * n + 1)
                        pool.tensor_copy(cnt[:, u:u + 1], cntm[0:1, :]).then_inc(cnt_step, 1)
                    if g > 0 and phase == 0:
                        ka = ((g - 1) * 2 + img) * 8 + k
                        own_wait(pool, y_out, 8 * ls + 8 + 1)
                        pool.tensor_copy(atab[:, bass.ds(k, 1), :].rearrange("p a k -> p (a k)"), yacc[:, u, :]
                                         ).then_inc(a_kept, 1)
                loop(pool, 8, body)

        @block.scalar
        def _(act):
            A = nc.scalar.activation
            for s in range(2):
                act.sem_inc(cur_free[s], 1)
                act.sem_inc(acc_free[s], 1)
            act.sem_inc(pst_free, 1)
            act_in = 0

            def small_fn(out_, in_, fn, **kw):
                nonlocal act_in
                act_in += 1
                act.wait_ge(to_act, act_in)
                A(out_, in_, fn, **kw).then_inc(act_small, 1)

            act.wait_ge(pe_small, 1)
            A(kk[:, :], small[:, 0:TAPS], ACT.Exp, scale=-E_EXP).then_inc(act_small, 1)
            act.wait_ge(filled, 4)
            act_in += 1
            act.wait_ge(to_act, act_in)
            A(krow_o[:, TAPS:2 * TAPS], krow_o[:, TAPS:2 * TAPS], ACT.Exp, scale=BETA,
              bias=col[0:32, C_EK:C_EK + 1]).then_inc(tabs_small, 1)
            small_fn(cc(W_NORM), cc(W_NORM), ACT.Sqrt)

            def stat_tile(g):
                def body(i2, u):
                    n = g * C + 2 * i2 + u
                    act.wait_ge(pst_in, 16 * n + 16)
                    A(pst[:, :], pst[:, :], ACT.Identity, scale=-1.0 / BLK, accum_out=pacc[:, u, 1:2]
                      ).then_inc(ps_step, 1)
                    act.wait_ge(ps_step, 3 * n + 1)
                    A(pst[:, :], pst[:, :], ACT.Square, scale=-float(BLK), bias=pacc[:, u, 1:2],
                      accum_out=pacc[:, u, 2:3]).then_inc(ps_step, 1)
                    own_wait(act, ps_step, 3 * n + 2)
                    act.sem_inc(pst_free, 1)
                    for f in range(2):
                        last = A(px[f][:, bass.ds(2 * i2 + u, 1)], pacc[:, u, f + 1:f + 2], ACT.Identity)
                    last.then_inc(ps_step, 1)
                return body

            loop(act, C, stat_tile(0))
            for g, blk in schedule():
                img, phase = divmod(blk, 2)
                if blk == 0 and g > 0:
                    small_fn(st[:, 5, :], st[:, 4, :], ACT.Sqrt)
                if blk == 0 and g < PAIRS:
                    small_fn(st[:, 5, :], st[:, 4, :], ACT.Sqrt)
                    act_in += 1
                    act.wait_ge(to_act, act_in)
                if g > 0 and phase == 0:
                    act_in += 1
                    act.wait_ge(to_act, act_in)
                if g > 0 and phase == 1:
                    small_fn(cc(GATE), cc(REL), ACT.Tanh, scale=0.5)
                    act_in += 1
                    act.wait_ge(to_act, act_in)

                def body(i, u, g=g, blk=blk, img=img, phase=phase):
                    i2 = 4 * blk + i
                    n = g * C + 2 * i2 + u
                    c = 2 * i2 + u
                    k = 2 * i + u
                    ls = ((g - 1) * 4 + blk) * 8 + k

                    def exp_sum(j, src, scale, bias, col_):
                        act.wait_ge(junk_w, 6 * n + j + 1)
                        ins = A(junk[:, 0:src.shape[1]], src, ACT.Exp, scale=cur[:, u, scale:scale + 1],
                                bias=cur[:, u, bias:bias + 1], accum_out=ex[:, u, col_:col_ + 1])
                        ins.then_inc(junk_w, 1)
                        return ins

                    def y_evac(e):
                        s = e // NCH
                        act.wait_ge(y_ready, 8 * ls + e + 1)
                        if phase == 0:
                            A(ps_y[:, :], ps_y[:, :], ACT.Square, bias=cc(BIASV),
                              accum_out=yacc[:, u, e:e + 1]).then_inc(y_out, 1)
                        else:
                            A(at[s][:, e % NCH * CH:(e % NCH + 1) * CH], ps_y[:, :], ACT.Identity,
                              bias=cc(BIASO)).then_inc(y_out, 1)

                    if g < PAIRS:
                        act.wait_ge(cur_set, n + 1)
                        act.wait_ge(x_in[u], LOADS * (g * (C // 2) + i2 + 1))
                        half = HR // 2 * HC
                        exp_sum(0, xt[u][:, 0:half], 3, 4, 0)
                        exp_sum(1, xt[u][:, half:2 * half], 3, 4, 1)
                    if g > 0 and phase == 1:
                        for e in range(NCH):
                            y_evac(e)
                        act.wait_ge(y_out, 8 * ls + NCH + 1)
                        act.sem_inc(at_free[0], 1)
                        act.dma_start(tile_of(out, 2 * (g - 1) + img, 2 * k + 0), at[0][:, :]
                                      ).then_inc(out_st[0], 16)
                    if g < PAIRS:
                        act.wait_ge(tap_done, TAPS * n + FIRST + 1)
                        exp_sum(2, accf[:, 0:BLK // 2], 5, 6, 2)
                        exp_sum(3, accf[:, BLK // 2:BLK], 5, 6, 3)
                        act.wait_ge(junk_w, 6 * n + 4 + 1)
                        act.sem_inc(sums_in, 1)
                    if g > 0 and phase == 1:
                        for e in range(NCH, 2 * NCH):
                            y_evac(e)
                        act.wait_ge(y_out, 8 * ls + 2 * NCH + 1)
                        act.sem_inc(at_free[1], 1)
                        act.dma_start(tile_of(out, 2 * (g - 1) + img, 2 * k + 1), at[1][:, :]
                                      ).then_inc(out_st[1], 16)
                    if g > 0 and phase == 0:
                        ka = ((g - 1) * 2 + img) * 8 + k
                        act.wait_ge(a_kept, ka + 1)
                        for s in range(2):
                            act.wait_ge(z_ready, 2 * ka + s + 1)
                            A(gates[:, bass.ds((2 * k + s) * MT, MT)], ps_t[:, 0:MT], ACT.Tanh, scale=0.5,
                              bias=cc(BIASZ)).then_inc(z_out, 1)
                            for e in range(NCH * s, NCH * s + NCH):
                                y_evac(e)
                            act.wait_ge(y_out, 8 * ls + 4 * s + 4 + 1)
                            act.sem_inc(at_free[s], 1)
                    if g < PAIRS - 1:
                        stat_tile(g + 1)(i2, u)
                    if g < PAIRS:
                        for e in range(NCH):
                            act.wait_ge(mix_ready, 4 * n + e + 1)
                            A(acc[u][:, e * CH:(e + 1) * CH], ps_mix[:, :], ACT.Identity, bias=cur[:, u, 2:3],
                              accum_out=xacc[:, u, e:e + 1]).then_inc(mix_out, 1)
                        act.wait_ge(mix_out, 4 * n + 4 + 1)
                        act.sem_inc(cur_free[u], 1)
                        dst = x1_d.rearrange("b c h w -> c b h w")[bass.ds(c, 1), 2 * g:2 * g + 2, :, :]
                        for q in range(QUARTERS):
                            for m in range(2):
                                act.dma_start(dst[0, m, :, q * TC:(q + 1) * TC].rearrange("(b r) c -> b r c", r=TR),
                                              acc[u][32 * q + m:32 * q + 32:2, :].rearrange("p (r c) -> p r c", c=TC)
                                              ).then_inc(x1_st[u], 16)
                        A(xacc[:, u, 0:4], xacc[:, u, 0:4],
                          ACT.Identity, scale=-1.0 / BLK, accum_out=xacc[:, u, 5:6]).then_inc(xs_step, 1)
                        act.wait_ge(xs_step, 4 * n + 1 + 1)
                        for j in range(2):
                            act.wait_ge(junk_w, 6 * n + 4 + j + 1)
                            A(junk[:, 0:BLK // 2], acc[u][:, j * BLK // 2:(j + 1) * BLK // 2], ACT.Square,
                              bias=xacc[:, u, 5:6], accum_out=xacc[:, u, j:j + 1]).then_inc(junk_w, 1)
                        act.wait_ge(junk_w, 6 * n + 6 + 1)
                        A(xacc[:, u, 0:2], xacc[:, u, 0:2], ACT.Identity, accum_out=xacc[:, u, 7:8]
                          ).then_inc(xs_step, 1)
                        own_wait(act, xs_step, 4 * n + 2 + 1)
                        for f in range(2):
                            A(p1[f][:, bass.ds(c, 1)], xacc[:, u, 5 + 2 * f:6 + 2 * f], ACT.Identity
                              ).then_inc(xs_step, 1)
                        own_wait(act, csum_ready, n + 1 + 1)
                        A(csum[:, bass.ds(c, 1), :].rearrange("p a k -> p (a k)"), ps_col[:, 0:2], ACT.Identity
                          ).then_inc(csum_out, 1)
                        act.sem_inc(acc_free[u], 1)
                loop(act, 8, body)
            for s in range(2):
                act.wait_ge(out_st[s], 16 * 8 * B + 1)

        @block.tensor
        def _(pe):
            M = nc.tensor.matmul
            for s in range(2):
                pe.sem_inc(x_free[s], 1)
            ins = 0

            def wait_operands():
                nonlocal ins
                ins += 1
                pe.wait_ge(to_pe, ins)

            def rep(a):
                return a.unsqueeze(1).to_broadcast([a.shape[0], QUARTERS, 32])

            pe.wait_ge(const_in, 16 * CONSTS)
            pe.wait_ge(filled, 1)
            M(small[:, 0:TAPS], fpt[:, :], basis[:, :], start=True, stop=True).then_inc(pe_small, 1)
            wait_operands()
            M(small[0:32, 0:2 * TAPS], const("fold"), sums[:, :], start=True, stop=True).then_inc(pe_small, 1)
            for i in range(4):
                wait_operands()
                M(small[:, 0:P], wraw[:, i, :], rep(ident[0:32, 0:32]), start=True, stop=True
                  ).then_inc(pe_small, 1)
            wait_operands()
            M(small[:, 0:P], wckr[:, :], ones[0:1, :], start=True, stop=True).then_inc(pe_small, 1)
            wait_operands()
            M(small[:, 0:1], wck, ones[:, 0:1], start=True, stop=True)
            M(small[:, 1:2], wck, cc(WCOL), start=True, stop=True)
            M(small[0:32, 2:3], wraw[:, 4, 0:32], ones[0:32, 0:1], start=True, stop=True).then_inc(pe_small, 1)

            def stats():
                for _ in range(2):
                    wait_operands()
                    M(small[:, 0:C], const("same"), st[:, 0, :], start=True, stop=True).then_inc(pe_small, 1)

            for g, blk in schedule():
                img, phase = divmod(blk, 2)
                if blk == 0 and g > 0:
                    stats()
                    wait_operands()
                    for f in range(4):
                        last = M(small[:, 2 * f:2 * f + 2], tb4[:, f, :, :].rearrange("p q c -> p (q c)"), ident[:, 0:2], start=True, stop=True)
                    for m in range(2):
                        last = M(small[0:32, 32 * m + 32:32 * m + 64], csum[:, :, m], const("fold"), start=True, stop=True)
                    last.then_inc(pe_small, 1)
                if blk == 0 and g < PAIRS:
                    stats()
                if g > 0 and phase == 0:
                    wait_operands()
                    M(small[:, 0:1], wv[:, :], cols[:, 0, img:img + 1], start=True, stop=True)
                    M(small[:, 1:2], wsq, cc(RM), start=True, stop=True).then_inc(pe_small, 1)
                    wait_operands()
                    M(small[:, 0:BW], ones[0:32, :], pp[:, :], start=True, stop=True).then_inc(pe_small, 1)
                    pe.wait_ge(wj_set, 2 * (g - 1) + img + 1)
                if g > 0 and phase == 1:
                    wait_operands()
                    M(small[:, 0:1], const("qfold"), cc(ASUM), start=True, stop=True).then_inc(pe_small, 1)
                    wait_operands()
                    M(small[:, 0:1], wckp, cc(ZC), start=True, stop=True).then_inc(pe_small, 1)
                    wait_operands()
                    M(small[:, 0:1], wcq, cc(UC), start=True, stop=True)
                    M(small[:, 1:2], wck, cols[:, 3, img:img + 1], start=True, stop=True).then_inc(pe_small, 1)
                    wait_operands()
                    M(small[:, 0:1], wa[:, :], cols[:, 0, img:img + 1], start=True, stop=True
                      ).then_inc(pe_small, 1)

                def body(i, u, g=g, blk=blk, img=img, phase=phase):
                    i2 = 4 * blk + i
                    n = g * C + 2 * i2 + u
                    k = 2 * i + u
                    ls = ((g - 1) * 4 + blk) * 8 + k
                    if g > 0 and phase == 0:
                        ka = ((g - 1) * 2 + img) * 8 + k
                        for s in range(2):
                            pe.wait_ge(z_out, 2 * ka + s + 1)
                            pe.wait_ge(at_in[s], 16 * (ls + 1))
                            runs = at[s][:, :].rearrange("p (m j) -> p j m", j=BW)
                            for j in range(BW):
                                last = M(ps_t[:, 0:MT], wj[:, j, :], runs[:, j, :], start=(j == 0), stop=(j == BW - 1))
                            last.then_inc(z_ready, 1)
                            for e in range(NCH * s, NCH * s + NCH):
                                pe.wait_ge(y_out, 8 * ls + e + 1)
                                for h in range(2):
                                    lo = e % NCH * CH + 512 * h
                                    last = M(ps_y[:, 512 * h:512 * h + 512], wv[:, :], at[s][:, lo:lo + 512],
                                             start=True, stop=True)
                                last.then_inc(y_ready, 1)
                    if g > 0 and phase == 1:
                        kb = ((g - 1) * 2 + img) * 8 + k

                        def spread(e):
                            q = e // 2
                            pe.wait_ge(gx_ready, 8 * kb + e + 1)
                            for h in range(2):
                                lo = e % 2 * CH + 512 * h
                                last = M(ps_g[:, 512 * h:512 * h + 512], selk[32 * q:32 * q + 32, u, :],
                                         gates[32 * q:32 * q + 32, lo:lo + 512], start=True, stop=True)
                            last.then_inc(g_ready, 1)

                        pe.wait_ge(selk_set, kb + 1)
                        spread(0)
                        for e in range(2 * NCH):
                            if e % NCH == 0:
                                pe.wait_ge(at_in[e // NCH], 16 * (ls + 1))
                            if e + 1 < 2 * NCH:
                                spread(e + 1)
                            pe.wait_ge(y_out, 8 * ls + e + 1)
                            pe.wait_ge(gx_ready, 8 * kb + e + 1 + 1)
                            for h in range(2):
                                lo = e % NCH * CH + 512 * h
                                yh = ps_y[:, 512 * h:512 * h + 512]
                                M(yh, wa[:, :], at[e // NCH][:, lo:lo + 512], start=True, stop=False)
                                last = M(yh, wb[:, :], gx[:, e % 2, 512 * h:512 * h + 512], start=False, stop=True)
                            last.then_inc(y_ready, 1)
                    if g < PAIRS:
                        pe.wait_ge(diag_set, n + 1)
                        pe.wait_ge(tap_done, TAPS * (n + 1) + 1)
                        X = xt[u][:, 0:HR * HC].rearrange("p (r c) -> p r c", c=HC)
                        for e in range(NCH):
                            pe.wait_ge(mix_out, 4 * n + e + 1)
                            for h in range(2):
                                r0 = (e * CH + 512 * h) // TC
                                mh = ps_mix[:, 512 * h:512 * h + 512]
                                M(mh, ident, X[:, R + r0:R + r0 + 512 // TC, R:R + TC], start=True, stop=False)
                                last = M(mh, diag[:, u, :], acc[u][:, r0 * TC:r0 * TC + 512], start=False, stop=True)
                            last.then_inc(mix_ready, 1)
                        pe.wait_ge(mix_ready, 4 * n + 4)
                        pe.sem_inc(x_free[u], 1)
                        pe.wait_ge(csum_out, n + 1)
                        pe.wait_ge(mix_out, 4 * n + 4 + 1)
                        for r in range(TR):
                            last = M(ps_col[:, 0:2], acc[u][:, r * TC:(r + 1) * TC], const("img"),
                                     start=(r == 0), stop=(r == TR - 1))
                        last.then_inc(csum_ready, 1)
                loop(pe, 8, body)

        @block.vector
        def _(dve):
            V = nc.vector
            links = 0
            pe_n = 0
            act_n = 0

            def link(i):
                nonlocal links
                links += 1
                i.then_inc(dve_small, 1)
                dve.wait_ge(dve_small, links)

            def from_pe():
                nonlocal pe_n
                pe_n += 1
                dve.wait_ge(pe_small, pe_n)

            def from_act():
                nonlocal act_n
                act_n += 1
                dve.wait_ge(act_small, act_n)

            def ts(out_, in_, s1, s2, o0, o1=None):
                if o1 is None:
                    link(V.tensor_scalar(out_, in_, s1, None, o0))
                else:
                    link(V.tensor_scalar(out_, in_, s1, s2, o0, o1))

            def tt(out_, a, b, op):
                link(V.tensor_tensor(out_, a, b, op))

            def stt(out_, a, s, b, o0, o1):
                link(V.scalar_tensor_tensor(out_, a, s, b, o0, o1))

            dve.wait_ge(const_in, 16 * CONSTS)
            from_act()
            tt(kk[:, :], kk[:, :], const("radial"), ALU.mult)
            ts(kk[:, :], kk[:, :], -NEG, None, ALU.min)
            for q in range(QUARTERS):
                link(V.tensor_copy(kq[32 * q:32 * q + 32, :], kk[32 * q:32 * q + 32, q * QB:(q + 1) * QB]))
            big = [at[0][:, 0:QB * TAPS].rearrange("p (t v) -> p t v", t=QB),
                   at[1][:, 0:QB * TAPS].rearrange("p (t v) -> p t v", t=QB)]
            tie = accf[:, 0:QB * TAPS].rearrange("p (t v) -> p t v", t=QB)
            every = kk[:, :].unsqueeze(1).to_broadcast([P, QB, TAPS])
            own = kq[:, :].unsqueeze(2).to_broadcast([P, QB, TAPS])
            dve.wait_ge(tie_in, 16)
            tt(big[0], every, own, ALU.is_equal)
            tt(big[0], big[0], tie, ALU.mult)
            tt(big[1], every, own, ALU.is_lt)
            tt(big[0], big[0], big[1], ALU.add)
            link(V.tensor_reduce(rank[:, :], big[0], AX_X, ALU.add))
            hot = [at[0][:, 0:QB * TAPS].rearrange("p (v t) -> p v t", t=QB),
                   at[1][:, 0:QB * TAPS].rearrange("p (v t) -> p v t", t=QB)]
            tt(hot[0], const("iota").unsqueeze(2).to_broadcast([P, TAPS, QB]),
               rank[:, :].unsqueeze(1).to_broadcast([P, TAPS, QB]), ALU.is_equal)
            tt(hot[1], hot[0], kq[:, :].unsqueeze(1).to_broadcast([P, TAPS, QB]), ALU.mult)
            link(V.tensor_reduce(sums[:, 0:TAPS], hot[1], AX_X, ALU.add))
            tt(hot[1], hot[0], const("offq").unsqueeze(1).to_broadcast([P, TAPS, QB]), ALU.mult)
            link(V.tensor_reduce(sums[:, TAPS:2 * TAPS], hot[1], AX_X, ALU.add))
            for s in range(2):
                dve.sem_inc(at_free[s], 1)
            dve.sem_inc(to_pe, 1)
            from_pe()
            from_pe()
            link(V.tensor_copy(krow_o[:, 0:TAPS], small[0:32, 0:TAPS]))
            ts(krow_o[:, TAPS:2 * TAPS], small[0:32, 0:TAPS], KCAP, None, ALU.min)
            dve.sem_inc(to_act, 1)
            link(V.tensor_copy(orow_o[:, :], small[0:32, TAPS:2 * TAPS]))
            dve.sem_inc(tabs_small, 1)
            for w in (wsq, wcq, wf1, wf2):
                dve.sem_inc(to_pe, 1)
                from_pe()
                tt(w, small[:, 0:P], const("bd"), ALU.mult)
            dve.sem_inc(to_pe, 1)
            from_pe()
            link(V.tensor_copy(cc(WCOL), small[:, 0:1]))
            tt(wck, small[:, 0:P], const("bd"), ALU.mult)
            dve.sem_inc(to_pe, 1)
            from_pe()
            link(V.tensor_copy(cc(W_SUM), small[:, 0:1]))
            ts(cc(W_NORM), small[:, 1:2], 1e-30, None, ALU.add)
            link(V.tensor_copy(col[0:32, WS_SUM:WS_SUM + 1], small[0:32, 2:3]))
            dve.sem_inc(to_act, 1)
            from_act()
            ts(cc(TMP), cc(W_SUM), 0.0, 2.0, ALU.is_ge, ALU.mult)
            ts(cc(TMP), cc(TMP), -1.0, None, ALU.add)
            link(V.reciprocal(cc(W_INV), cc(W_NORM)))
            tt(cc(W_ALPHA), cc(W_INV), cc(TMP), ALU.mult)
            tt(cc(W_IALPHA), cc(W_NORM), cc(TMP), ALU.mult)
            ts(wckp, wck, cc(W_ALPHA), None, ALU.mult)
            tt(ipw, wckp, ident, ALU.add)
            tt(cc(TMP), cc(W_ALPHA), cc(W_SUM), ALU.mult)
            ts(cc(TMP), cc(TMP), 0.5, 1.0, ALU.mult, ALU.add)
            link(V.reciprocal(cc(W_IDEN), cc(TMP)))

            def stats(nmean, sq):
                ts(st[:, 0, :], nmean[:, :], -float(BLK), None, ALU.mult)
                dve.sem_inc(to_pe, 1)
                from_pe()
                link(V.tensor_copy(st[:, 2, :], small[:, 0:C]))

                def grouped(out_, in_, scale, bias):
                    pair = in_.rearrange("p (g a) -> p g a", a=2)
                    tt(st[:, 5, 0:GC], pair[:, :, 0], pair[:, :, 1], ALU.add)
                    ts(out_.rearrange("p (g a) -> p g a", a=2), st[:, 5, 0:GC].unsqueeze(2).to_broadcast([P, GC, 2]),
                       scale, bias, ALU.mult, ALU.add)

                grouped(st[:, 1, :], st[:, 2, :], 0.5 / HW, 0.0)
                stt(st[:, 3, :], nmean[:, :], 1.0, st[:, 1, :], ALU.mult, ALU.add)
                stt(st[:, 4, :], st[:, 3, :], float(BLK), st[:, 3, :], ALU.mult, ALU.mult)
                tt(st[:, 0, :], st[:, 4, :], sq[:, :], ALU.add)
                dve.sem_inc(to_pe, 1)
                from_pe()
                link(V.tensor_copy(st[:, 7, :], small[:, 0:C]))
                grouped(st[:, 4, :], st[:, 7, :], 0.5 / HW, EPS)
                dve.sem_inc(to_act, 1)
                from_act()
                link(V.reciprocal(st[:, 6, :], st[:, 5, :]))
                tt(st[:, 6, :], st[:, 6, :], st[:, 4, :], ALU.mult)
                tt(st[:, 3, :], st[:, 6, :], st[:, 5, :], ALU.add)
                ts(st[:, 3, :], st[:, 3, :], 0.5, None, ALU.mult)
                link(V.reciprocal(st[:, 6, :], st[:, 3, :]))

            def prepare_pair():
                stats(px[0], px[1])
                link(V.tensor_copy(stat[:, :, 0], st[:, 3, :]))
                link(V.tensor_copy(stat[:, :, 1], st[:, 6, :]))
                stt(stat[:, :, 2], st[:, 1, :], -1.0, st[:, 6, :], ALU.mult, ALU.mult)
                ts(stat[:, :, 3], st[:, 6, :], BETA, None, ALU.mult)
                ts(stat[:, :, 4], stat[:, :, 2], BETA, -OFFS, ALU.mult, ALU.add)
                ts(stat[:, :, 5], st[:, 6, :], -BETA, None, ALU.mult)
                ts(stat[:, :, 6], stat[:, :, 2], -BETA, -OFFS, ALU.mult, ALU.add)
                ts(stat[:, :, 7], st[:, 6, :], 0.0, None, ALU.mult)
                dve.sem_inc(to_pool, 1)
                dve.sem_inc(to_act, 1)

            def prepare_attention():
                stats(p1[0], p1[1])
                link(V.tensor_copy(tb[:, 0, :], st[:, 1, :]))
                link(V.tensor_copy(tb[:, 1, :], st[:, 6, :]))
                stt(st[:, 4, :], st[:, 1, :], -float(HW), st[:, 2, :], ALU.mult, ALU.add)
                tt(tb[:, 3, :], st[:, 4, :], st[:, 6, :], ALU.mult)
                tt(st[:, 4, :], st[:, 7, :], st[:, 6, :], ALU.mult)
                tt(tb[:, 2, :], st[:, 4, :], st[:, 6, :], ALU.mult)
                for q in range(QUARTERS):
                    link(V.tensor_copy(tb4[:, :, q, :], tb[:, :, :]))
                dve.sem_inc(to_pe, 1)
                from_pe()
                link(V.tensor_copy(cols[:, :, :].rearrange("p a b -> p (a b)"), small[:, 0:8]))
                link(V.tensor_copy(classes[:, :, :].rearrange("p a b -> p (a b)"), small[0:32, 32:96]))

            def prepare_gates(img):
                m, r = cols[:, 0, img:img + 1], cols[:, 1, img:img + 1]
                ts(wv[:, :], ipw, r, None, ALU.mult)
                tt(cc(RM), r, m, ALU.mult)
                dve.sem_inc(to_pe, 1)
                from_pe()
                ts(cc(BIASV), small[:, 0:1], -1.0, None, ALU.mult)
                tt(cc(BIASZ), bcol[:, 0:1], small[:, 1:2], ALU.subtract)
                ts(cc(TMP), m, float(HW // BW), None, ALU.mult)
                tt(cc(WRC)[0:32], cc(WS_SUM)[0:32], r[0:32], ALU.mult)
                ts(pp[:, :], classes[:, img, :], cc(TMP)[0:32], cc(WRC)[0:32], ALU.subtract, ALU.mult)
                ts(cc(TMP)[0:32], bcol[0:32, 4:5], float(HW // BW), None, ALU.mult)
                ts(pp[:, :], pp[:, :], cc(TMP)[0:32], None, ALU.add)
                dve.sem_inc(to_pe, 1)
                from_pe()
                ts(skb[:, :], small[:, 0:BW], 1.0 / HW, None, ALU.mult)
                link(V.tensor_reduce(cc(SKSUM), skb[:, :], AX_X, ALU.add))
                ts(skr[:, :], skb[:, :], r, None, ALU.mult)
                dve.sem_inc(to_pool, 1)
                ts(cc(BIASZ), cc(BIASZ), cc(SKSUM), 0.5, ALU.mult, ALU.mult)
                dve.sem_inc(to_act, 1)

            def prepare_output(g, img):
                m, r = cols[:, 0, img:img + 1], cols[:, 1, img:img + 1]
                b2, sh = cols[:, 2, img:img + 1], cols[:, 3, img:img + 1]
                dve.wait_ge(a_kept, 8 * (2 * (g - 1) + img + 1) + 1)
                dve.wait_ge(y_out, 8 * (8 * (4 * (g - 1) + 2 * img + 1)) + 1)
                link(V.tensor_reduce(cc(ASUM), atab[:, :, :].rearrange("p a b -> p (a b)"), AX_X, ALU.add))
                dve.sem_inc(to_pe, 1)
                from_pe()
                tt(cc(ZC), small[:, 0:1], b2, ALU.subtract)
                ts(cc(ZC), cc(ZC), 0.5, None, ALU.mult)
                dve.sem_inc(to_pe, 1)
                from_pe()
                tt(cc(KP), small[:, 0:1], cc(W_IDEN), ALU.mult)
                stt(cc(UC), cc(KP), -0.5, cc(ZC), ALU.mult, ALU.add)
                tt(cc(UC), cc(UC), cc(W_IALPHA), ALU.mult)
                stt(cc(UC), sh, bcol[:, 3:4], cc(UC), ALU.mult, ALU.add)
                dve.sem_inc(to_pe, 1)
                from_pe()
                stt(cc(TMP), bcol[:, 3:4], float(HW), small[:, 1:2], ALU.mult, ALU.add)
                tt(cc(TMP), cc(TMP), bcol[:, 1:2], ALU.mult)
                tt(cc(REL), small[:, 0:1], cc(TMP), ALU.add)
                dve.sem_inc(to_act, 1)
                from_act()
                ts(cc(GATE), cc(GATE), -0.5, 0.5, ALU.mult, ALU.add)
                tt(cc(RG), cc(GATE), r, ALU.mult)
                ts(cc(R5), r, 0.5, None, ALU.mult)
                ts(wtmp, wf2, cc(R5), None, ALU.mult)
                stt(wa[:, :], wf1, cc(RG), wtmp, ALU.mult, ALU.add)
                tt(wa[:, :], wa[:, :], ident, ALU.add)
                ts(wb[:, :], wtmp, -1.0, None, ALU.mult)
                dve.sem_inc(to_pe, 1)
                from_pe()
                tt(cc(TMP), bcol[:, 2:3], m, ALU.add)
                tt(cc(BIASO), cc(TMP), small[:, 0:1], ALU.subtract)
                dve.sem_inc(to_act, 1)

            for g, blk in schedule():
                img, phase = divmod(blk, 2)
                if blk == 0 and g > 0:
                    dve.wait_ge(xs_step, 4 * g * C + 1)
                    dve.wait_ge(csum_out, g * C + 1)
                    prepare_attention()
                if blk == 0 and g < PAIRS:
                    dve.wait_ge(ps_step, 3 * (g + 1) * C)
                    prepare_pair()
                if g > 0 and phase == 0:
                    prepare_gates(img)
                if g > 0 and phase == 1:
                    prepare_output(g, img)

                def body(i, u, g=g, blk=blk, img=img, phase=phase):
                    i2 = 4 * blk + i
                    n = g * C + 2 * i2 + u
                    k = 2 * i + u
                    ls = ((g - 1) * 4 + blk) * 8 + k
                    kb = ((g - 1) * 2 + img) * 8 + k

                    def gate_chunk(e):
                        if e % NCH == 0:
                            dve.wait_ge(at_in[e // NCH], 16 * (ls + 1))
                        if e >= 2:
                            dve.wait_ge(y_ready, 8 * ls + e - 1)
                        dve.wait_ge(g_ready, 8 * kb + e + 1 + 1)
                        V.scalar_tensor_tensor(gx[:, e % 2, :], at[e // NCH][:, e % NCH * CH:(e % NCH + 1) * CH],
                                               cols[:, 0, img:img + 1], ps_g[:, :], ALU.subtract, ALU.mult
                                               ).then_inc(gx_ready, 1)

                    if g == PAIRS:
                        if phase == 1:
                            for e in range(2 * NCH):
                                gate_chunk(e)
                        return

                    def shifted(off):
                        return xt[u][:, bass.ds(off, TR * HC)].rearrange("p (r c) -> p r c", c=HC)[:, :, 0:TC]

                    def block_of(a):
                        return a[:, :].rearrange("p (r c) -> p r c", c=TC)

                    def offsets(t0, count):
                        return nc.values_load_multi_w_load_instructions(
                            orow[0:1, u, bass.ds(t0, count)], engines=[mybir.EngineType.DVE], min_val=0,
                            max_val=2 * R * HC + 2 * R,
                            skip_runtime_bounds_check_because="a permutation of the table of offsets")[1]

                    dve.wait_ge(row_in[u], 32 * (g * (C // 2) + i2 + 1))
                    dve.wait_ge(cur_set, n + 1)
                    V.tensor_scalar(pen[:, u, :], krow[:, u, 0:TAPS], cur[:, u, 0:1], None, ALU.mult
                                    ).then_inc(pen_set, 1)
                    off = offsets(0, FIXED)
                    dve.wait_ge(x_in[u], LOADS * (g * (C // 2) + i2 + 1))
                    dve.wait_ge(sums_in, n + 1)
                    for t in range(FIXED):
                        if t == FIRST:
                            dve.wait_ge(x1_st[u], STORES * (g * (C // 2) + i2) + 1)
                            dve.wait_ge(acc_free[u], g * (C // 2) + i2 + 1)
                        before = CENTRE if t == 0 else None
                        in1 = shifted(CENTRE) if t == 0 else block_of(accf if t <= FIRST else acc[u])
                        if t == 0:
                            dve.wait_ge(pen_set, n + 1)
                        dve.wait_ge(tap_done, TAPS * n + t + 1)
                        V.scalar_tensor_tensor(block_of(accf if t < FIRST else acc[u]), shifted(off[t]),
                                               pen[:, u, t:t + 1], in1, ALU.subtract, ALU.max).then_inc(tap_done, 1)
                        if g > 0 and phase == 1 and t >= FIXED - 2 * NCH:
                            gate_chunk(t - (FIXED - 2 * NCH))
                        if t == COUNT_AT:
                            dve.wait_ge(bnd_step, 4 * n + 4)
                            V.tensor_scalar(flag[:, :], krow[:, u, TAPS:2 * TAPS], bnd[:, 0:1], 0.0, ALU.is_lt, ALU.add,
                                            accum_out=cntp[:, u:u + 1]).then_inc(counted, 1)
                    own_wait(dve, cnt_step, 2 * n + 2)
                    need = dve.value_load(cnt[0:1, u:u + 1], min_val=0, max_val=TAPS)

                    def tap_groups(lo, hi):
                        with dve.Fori(lo, hi) as grp:
                            t0 = FIXED + grp * GRP
                            with dve.If(t0 < need):
                                off = offsets(t0, GRP)
                                for j in range(GRP):
                                    def tap(j=j):
                                        dve.wait_ge(tap_done, TAPS * n + t0 + j + 1)
                                        V.scalar_tensor_tensor(
                                            block_of(acc[u]), shifted(off[j]), pen[:, u, bass.ds(t0 + j, 1)],
                                            block_of(acc[u]), ALU.subtract, ALU.max).then_inc(tap_done, 1)
                                    if j == 0:
                                        tap()
                                        continue
                                    with dve.If(t0 + j < need):
                                        tap()
                                    with dve.Else():
                                        dve.sem_inc(tap_done, 1)
                            with dve.Else():
                                dve.sem_inc(tap_done, GRP)

                    tap_groups(0, NEAR)
                    with dve.If(FIXED + NEAR * GRP < need):
                        tap_groups(NEAR, GROUPS)
                    with dve.Else():
                        dve.sem_inc(tap_done, (GROUPS - NEAR) * GRP)
                loop(dve, 8, body)


_INS = ["x", "L0_conv_finsler_params", "L1_conv_w_ck", "L1_conv_b_ck", "L1_conv_w_cq", "L1_conv_b_cq", "L1_conv_w_sk",
        "L1_conv_b_sk", "L1_conv_w_sq", "L1_conv_b_sq", "L1_conv_w_f", "L1_conv_b_f"]


def kernel(**inputs):
    import concourse.bacc as _bacc
    from concourse.bass_utils import run_bass_kernel_spmd as _run

    nc = _bacc.Bacc("TRN2", target_bir_lowering=False, num_devices=1)
    arrays, args = {}, []
    named = [(n, np.ascontiguousarray(inputs[n])) for n in _INS] + list(shape_constants().items())
    for name, a in named:
        arrays[f"in_{name}"] = a
        args.append(nc.dram_tensor(f"in_{name}", a.shape, mybir.dt.from_np(a.dtype), kind="ExternalInput").ap())
    args.append(nc.dram_tensor("out_0", (B, C, H, W), F32, kind="ExternalOutput").ap())
    build(nc, *args)
    r = _run(nc, [arrays], core_ids=[0])
    return r.results[0]["out_0"]
```

```python
from contextlib import ExitStack

import numpy as np

import concourse.bass as bass
from concourse import mybir

ALU = mybir.AluOpType
ACT = mybir.ActivationFunctionType
F32 = mybir.dt.float32
BF16 = mybir.dt.bfloat16
I32 = mybir.dt.int32
AX_X = mybir.AxisListType.X
RMAX = bass.bass_isa.ReduceOp.max

B, C, H, W = 8, 32, 512, 512
HW = H * W
P = 128
PAIRS = B // 2
R = 5
KS = 2 * R + 1
TAPS = KS * KS - 1
QUARTERS = 4
BANDS = P // (2 * QUARTERS)
TR, TC = H // BANDS, W // QUARTERS
HR, HC = TR + 2 * R, TC + 2 * R
BLK = TR * TC
XLEN = HR * HC + 12
CENTRE = R * HC + R
GC = 16
EPS = 1e-5
NEG = -1e30
ALPHA = 0.65
E_EXP = 2.0 * ALPHA / (2.0 * ALPHA - 1.0)
NU = (2.0 * ALPHA - 1.0) * (2.0 * ALPHA) ** (-E_EXP)
FIRST = 12
FIXED = 20
HOOK_AT = 7
COUNT_AT = 14
GATE_AT = (8, 9, 10, 12, 13, 15, 16, 17)
EARLY = 3
GRP = 10
NEAR = 3
GROUPS = (TAPS - FIXED) // GRP
BETA = 8.0
OFFS = 24.0
KCAP = 16.5
AT = 4096
CH = 1024
NCH = AT // CH
LOADS = 16 * 4 * QUARTERS
STORES = 16 * 2 * QUARTERS
BW = 32
MT = AT // BW
QB = TAPS // QUARTERS

CONSTS = 2 + 5 * 4 + 2 * 4 + 3 * 4 + 2

_W = dict(ident=P, same=P, qfold=P, bd=P, img=2, fold=32, sel=8 * P, iota=TAPS, radial=TAPS, offq=QB)
CO, _at = {}, 0
for _k, _n in _W.items():
    CO[_k] = (_at, _at + _n)
    _at += _n
NCONST = _at


def shape_constants():
    p = np.arange(P)
    c = np.zeros((P, NCONST), np.float32)

    def put(name, a):
        c[:, CO[name][0]:CO[name][1]] = a

    put("ident", p[:, None] == p[None, :])
    put("same", p[:, None] % 2 == p[None, :] % 2)
    put("qfold", p[:, None] % 32 == p[None, :] % 32)
    put("bd", p[:, None] // 32 == p[None, :] // 32)
    put("img", p[:, None] % 2 == np.arange(2)[None, :])
    put("fold", p[:, None] % 32 == np.arange(32)[None, :])
    k = np.arange(8)
    put("sel", ((p[:, None, None] % 32) == (p[None, None, :] // 32) * 8 + k[None, :, None]).reshape(P, -1))
    put("iota", np.arange(TAPS)[None, :])
    d = np.arange(-R, R + 1)
    yy, xx = (a.reshape(-1) for a in np.meshgrid(d, d, indexing="ij"))
    keep = (yy != 0) | (xx != 0)
    yy, xx = yy[keep], xx[keep]
    rho, theta = np.sqrt(yy * yy + xx * xx), np.arctan2(yy, xx)
    put("radial", (NU * rho ** E_EXP)[None, :])
    off = (yy + R) * HC + xx + R
    put("offq", off.reshape(QUARTERS, QB)[p // 32])
    basis = np.stack([np.cos((m + 1) // 2 * theta) if m % 2 else np.sin((m + 1) // 2 * theta)
                      for m in range(1, 7)]).astype(np.float32)
    t = (p // 32)[:, None] * QB + np.arange(QB)[None, :]
    tie = (np.arange(TAPS)[None, None, :] < t[:, :, None]).astype(np.float32).reshape(P, -1)
    return {"cst": c, "basis": basis, "tie": tie}


def build(nc, x, fp, w_ck, b_ck, w_cq, b_cq, w_sk, b_sk, w_sq, b_sq, w_f, b_f, cst_d, basis_d, tie_d, out):
    x1_d = nc.dram_tensor("x1_scratch", [B, C, H, W], F32, kind="Internal").ap()
    ktab_d = nc.dram_tensor("ktab_scratch", [C, 2 * TAPS], F32, kind="Internal").ap()
    otab_d = nc.dram_tensor("otab_scratch", [C, TAPS], I32, kind="Internal").ap()

    with ExitStack() as ctx:
        def sb(name, shape, dt=F32):
            return ctx.enter_context(nc.sbuf_tensor(name, shape, dt))

        def sem(name):
            return ctx.enter_context(nc.semaphore(name))

        xt = [sb(f"xt{s}", [P, XLEN]) for s in range(2)]
        accf = sb("acc_first", [P, BLK])
        acc = [sb(f"acc{s}", [P, BLK]) for s in range(2)]
        junk = sb("junk", [P, (TR // 2 + 2 * R) * HC], BF16)
        pst = sb("stat_tile", [P, BLK])
        at = [sb(f"att{s}", [P, AT]) for s in range(2)]
        gxf = sb("gated", [P, 2 * CH])
        gx = gxf[:, :].rearrange("p (s f) -> p s f", s=2)
        gates = sb("gates", [P, HW // BW // QUARTERS])
        wj = sb("w_spatial", [P, BW, P])
        krow = sb("krow", [P, 2, 2 * TAPS])
        orow = sb("orow", [1, 2, TAPS], I32)
        pen = sb("pen", [P, 2, TAPS])
        flag = sb("flag", [P, TAPS])
        cst = sb("cst_sb", [P, NCONST])
        cur = sb("cur", [P, 2, 8])
        diag = sb("diag", [P, 2, P])
        selk = sb("selk", [P, 2, P])
        ex = sb("ex", [P, 2, 4])
        bnd = sb("bnd", [P, 7])
        cntp = sb("cntp", [P, 2])
        cntm = sb("cntm", [P, 1])
        cnt = sb("cnt", [1, 2], I32)
        pacc = sb("pacc", [P, 2, 3])
        xacc = sb("xacc", [P, 2, 8])
        yacc = sb("yacc", [P, 2, 8])
        stat = sb("stat", [P, C, 8])
        px = [sb(f"px{i}", [P, C]) for i in range(2)]
        p1 = [sb(f"p1{i}", [P, C]) for i in range(2)]
        csum = sb("csum", [P, C, 2])
        atab = sb("atab", [P, 8, 8])
        tb = sb("tb", [P, 4, C])
        tb4 = sb("tb4", [P, 4, QUARTERS, C])
        cols = sb("cols", [P, 4, 2])
        st = sb("st", [P, 8, C])
        wf = sb("weights", [P, 9, P])
        wsq, wcq, wf1, wf2, wck, wckp, ipw, wtmp = (wf[:, i, :] for i in range(8))
        wv, wa, wb = (sb(n, [P, P]) for n in ("wv", "wa", "wb"))
        bcol = sb("bcol", [P, 5])
        ones = sb("ones", [P, P])
        carved = 0

        def carve(rows, n):
            nonlocal carved
            carved += n
            return gxf[0:rows, carved - n:carved]

        wraw = carve(32, 5 * P).rearrange("p (i m) -> p i m", i=5)
        wckr, fpt, basis = carve(1, P), carve(6, P), carve(6, TAPS)
        kk, kq, rank, sums = (carve(P, n) for n in (TAPS, QB, QB, 2 * TAPS))
        krow_o, orow_o = carve(32, 2 * TAPS), carve(32, TAPS).bitcast(I32)
        col = sb("col", [P, 24])
        skb = sb("skb", [P, BW])
        skr = sb("skr", [P, BW])
        classes = sb("classes", [32, 2, BW])
        pp = sb("pp", [32, BW])
        (W_SUM, W_NORM, W_INV, W_ALPHA, W_IALPHA, W_IDEN, WS_SUM, RM, BIASV, BIASZ, SKSUM, ASUM, ZC, KP, UC,
         REL, GATE, RG, R5, BIASO, TMP, WCOL, WRC, C_EK) = range(24)

        def cc(i):
            return col[:, i:i + 1]

        def const(name):
            return cst[:, CO[name][0]:CO[name][1]]

        ident = const("ident")
        sel = const("sel").rearrange("p (k m) -> p k m", k=8)

        ps_mix = ctx.enter_context(nc.psum_tensor("ps_mix", [P, CH], F32))
        ps_y = ctx.enter_context(nc.psum_tensor("ps_y", [P, CH], F32))
        ps_g = ctx.enter_context(nc.psum_tensor("ps_g", [P, CH], F32))
        ps_col = ctx.enter_context(nc.psum_tensor("ps_col", [P, 512], F32))
        ps_t = ctx.enter_context(nc.psum_tensor("ps_t", [P, 512], F32))

        def y_bank(g, e):
            return (ps_mix if g == PAIRS and e % 2 else ps_y), (2 if g == PAIRS else 1)

        small = ps_t[:, P:512]

        const_in = sem("const_in")
        tie_in = sem("tie_in")
        filled = sem("filled")
        tabs_out = sem("tabs_out")
        x_in = [sem(f"x_in{s}") for s in range(2)]
        row_in = [sem(f"row_in{s}") for s in range(2)]
        x_free = [sem(f"x_free{s}") for s in range(2)]
        cur_free = [sem(f"cur_free{s}") for s in range(2)]
        cur_set = sem("cur_set")
        diag_set = sem("diag_set")
        pen_set = sem("pen_set")
        tap_done = sem("tap_done")
        junk_w = sem("junk_w")
        sums_in = sem("sums_in")
        bnd_step = sem("bnd_step")
        counted = sem("counted")
        cnt_step = sem("cnt_step")
        mix_ready = sem("mix_ready")
        mix_out = sem("mix_out")
        xs_step = sem("xs_step")
        csum_ready = sem("csum_ready")
        csum_out = sem("csum_out")
        acc_free = [sem(f"acc_free{s}") for s in range(2)]
        x1_st = [sem(f"x1_st{s}") for s in range(2)]
        pre = (pst, acc[0])
        pre_in = [sem(f"pre_in{s}") for s in range(2)]
        pre_free = [sem(f"pre_free{s}") for s in range(2)]
        pst_in = sem("pst_in")
        pst_free = sem("pst_free")
        ps_step = sem("ps_step")
        at_in = [sem(f"at_in{s}") for s in range(2)]
        at_free = [sem(f"at_free{s}") for s in range(2)]
        z_ready = sem("z_ready")
        z_out = sem("z_out")
        y_ready = sem("y_ready")
        y_out = sem("y_out")
        a_kept = sem("a_kept")
        g_ready = sem("g_ready")
        gx_ready = sem("gx_ready")
        selk_set = sem("selk_set")
        wj_set = sem("wj_set")
        out_st = [sem(f"out_st{s}") for s in range(2)]
        to_pe = sem("to_pe")
        to_act = sem("to_act")
        to_pool = sem("to_pool")
        pe_small = sem("pe_small")
        act_small = sem("act_small")
        dve_small = sem("dve_small")
        passed = sem("passed")
        tabs_small = sem("tabs_small")

        block = ctx.enter_context(nc.Block())

        def loop(eng, count, body, hook=None, late=None):
            if hook is not None:
                body(0, 0, hook)
                body(0, 1)
            with eng.Fori(0 if hook is None else 1, count // 2 - (late is not None)) as i:
                for u in range(2):
                    body(i, u)
            if late is not None:
                body(count // 2 - 1, 0)
                body(count // 2 - 1, 1, late=late)

        def own_wait(eng, semaphore, value):
            eng.wait_ge(semaphore, value)
            eng.sem_inc(passed, 1)


        def schedule():
            for g in range(PAIRS + 1):
                for blk in range(4):
                    yield g, blk

        def halo_loads(eng, g, c, s):
            X = xt[s][:, 0:HR * HC].rearrange("p (r c) -> p r c", c=HC)
            img = x.rearrange("b c h w -> c b h w")
            for q in range(QUARTERS):
                lo = R if q == 0 else 0
                hi = HC - R if q == QUARTERS - 1 else HC
                col0 = q * TC - R + lo
                n = hi - lo
                src = img[bass.ds(c, 1), 2 * g:2 * g + 2, :, :]
                p0 = 32 * q
                eng.dma_start(X[p0:p0 + 2, R:HR, lo:hi],
                              src[0, :, 0:TR + R, col0:col0 + n]).then_inc(x_in[s], 16)
                for m in range(2):
                    base = src[0, m, TR - R:TR - R + HR, col0:col0 + n]
                    mid = bass.AP(base.tensor, base.offset, [[TR * W, BANDS - 2], [W, HR], [1, n]])
                    eng.dma_start(X[p0 + 2 + m:p0 + 30:2, :, lo:hi], mid).then_inc(x_in[s], 16)
                eng.dma_start(X[p0 + 30:p0 + 32, 0:TR + R, lo:hi],
                              src[0, :, H - TR - R:H, col0:col0 + n]).then_inc(x_in[s], 16)

        def stat_load(eng, g, c, dst, landed):
            base = x.rearrange("b c h w -> c b (h w)")[bass.ds(c, 1), 2 * g:2 * g + 2, 0:BLK]
            src = bass.AP(base.tensor, base.offset, [[BLK, HW // BLK], [C * HW, 2], [1, BLK]])
            eng.dma_start(dst[:, :], src).then_inc(landed, 16)

        from_one = (tap_done, sums_in, csum_out, csum_ready, xs_step, junk_w, mix_out, y_out, z_out, gx_ready, a_kept,
                    g_ready, x1_st[0], x1_st[1], out_st[0], out_st[1])

        def tile_of(a, b, t):
            base = a[b].rearrange("c h w -> c (h w)")[:, bass.ds(t * AT, AT)]
            return bass.AP(base.tensor, base.offset, [[HW // QUARTERS, QUARTERS], [HW, C], [1, AT]])

        @block.sync
        def _(sp):
            for s in from_one:
                sp.sem_inc(s, 1)
            sp.dma_start(cst[:, :], cst_d).then_inc(const_in, 16)
            sp.dma_start(basis[:, :], basis_d).then_inc(const_in, 16)
            for i, (w, lo) in enumerate(((w_sq, 0), (w_cq, 0), (w_f, 0), (w_f, 32), (w_sk, 0))):
                for q in range(QUARTERS):
                    sp.dma_start(wraw[:, i, 32 * q:32 * q + 32], w[:, lo:lo + 32]).then_inc(const_in, 16)
            with nc.allow_non_contiguous_dma("a few hundred elements, once"):
                for q in range(QUARTERS):
                    sp.dma_start(wckr[:, 32 * q:32 * q + 32], w_ck).then_inc(const_in, 16)
                    sp.dma_start(fpt[:, 32 * q:32 * q + 32], fp.rearrange("c k -> k c")).then_inc(const_in, 16)
                for i, b in enumerate((b_sq, b_cq, b_f)):
                    for q in range(4):
                        sp.dma_start(bcol[32 * q:32 * q + 32, i:i + 1],
                                     b.rearrange("(c a) -> c a", a=1)).then_inc(const_in, 16)
                sp.dma_start(bcol[:, 3:4], bass.AP(b_ck.tensor, b_ck.offset, [[0, P], [1, 1]])).then_inc(const_in, 16)
                sp.dma_start(bcol[0:32, 4:5], b_sk.rearrange("(c a) -> c a", a=1)).then_inc(const_in, 16)
            sp.dma_start(accf[:, 0:QB * TAPS], tie_d).then_inc(tie_in, 16)
            def first_stat(i, u):
                sp.wait_ge(pre_free[u], i + 1)
                stat_load(sp, 0, 2 * i + u, pre[u], pre_in[u])

            loop(sp, C, first_stat)
            sp.wait_ge(tabs_small, 2)
            sp.dma_start(ktab_d, krow_o[:, :]).then_inc(tabs_out, 16)
            sp.dma_start(otab_d, orow_o[:, :]).then_inc(tabs_out, 16)
            sp.wait_ge(tabs_out, 32)
            sp.wait_ge(filled, 4)
            for g, blk in schedule():
                img, phase = divmod(blk, 2)
                if g > 0 and blk == 0:
                    for s in range(2):
                        sp.wait_ge(x1_st[s], STORES * (C // 2) * g + 1)

                def attention_loads(i, u, g=g, blk=blk, img=img, phase=phase):
                    k = 2 * i + u
                    ls = ((g - 1) * 4 + blk) * 8 + k
                    stored = ((g - 1) * 2 + img) * 8 + (k if phase == 1 else 0)
                    for s in range(2):
                        sp.wait_ge(at_free[s], ls + 1)
                        sp.wait_ge(out_st[s], 16 * stored + 1)
                        sp.dma_start(at[s][:, :], tile_of(x1_d, 2 * (g - 1) + img, 2 * k + s)).then_inc(at_in[s], 16)

                def body(i, u, g=g, blk=blk):
                    if g == PAIRS:
                        attention_loads(i, u)
                        return
                    i2 = 4 * blk + i
                    c = 2 * i2 + u
                    sp.wait_ge(x_free[u], g * (C // 2) + i2 + 1)
                    krs = bass.AP(ktab_d.tensor, 0, [[2 * TAPS, C], [1, 2 * TAPS]])[bass.ds(c, 1), :]
                    sp.dma_start(krow[:, u, :], bass.AP(krs.tensor, krs.offset, [[0, P], [1, 2 * TAPS]])
                                 ).then_inc(row_in[u], 16)
                    sp.dma_start(orow[:, u, :], otab_d[bass.ds(c, 1), :]).then_inc(row_in[u], 16)
                    halo_loads(sp, g, c, u)
                    if g > 0:
                        attention_loads(i, u)
                    if g + 1 < PAIRS:
                        sp.wait_ge(pst_free, g * C + 2 * i2 + u + 1)
                        stat_load(sp, g + 1, 2 * i2 + u, pst, pst_in)
                loop(sp, 8, body)

        @block.gpsimd
        def _(pool):
            pool.memset(ones[:, :], 1.0).then_inc(filled, 1)
            pool.memset(xt[0][:, :], NEG).then_inc(filled, 1)
            pool.memset(xt[1][:, :], NEG).then_inc(filled, 1)
            pool.memset(cc(C_EK), -2.0 * OFFS).then_inc(filled, 1)

            to_pool_n = 0
            for g, blk in schedule():
                img, phase = divmod(blk, 2)
                if blk == 0 and g < PAIRS:
                    to_pool_n += 1
                    pool.wait_ge(to_pool, to_pool_n)
                def keys():
                    nonlocal to_pool_n
                    to_pool_n += 1
                    pool.wait_ge(to_pool, to_pool_n)
                    pool.tensor_tensor(wj[:, :, :], wsq.unsqueeze(1).to_broadcast([P, BW, P]),
                                       skr[:, :].unsqueeze(2).to_broadcast([P, BW, P]), ALU.mult).then_inc(wj_set, 1)

                def body(i, u, hook=None, late=None, g=g, blk=blk, img=img, phase=phase):
                    i2 = 4 * blk + i
                    n = g * C + 2 * i2 + u
                    c = 2 * i2 + u
                    if g < PAIRS:
                        own_wait(pool, cur_free[u], g * (C // 2) + i2 + 1)
                        pool.tensor_copy(cur[:, u, :], stat[:, bass.ds(c, 1), :].rearrange("p a k -> p (a k)")
                                         ).then_inc(cur_set, 1)
                        own_wait(pool, cur_set, n + 1)
                        pool.tensor_scalar(diag[:, u, :], ident, cur[:, u, 1:2], None, ALU.mult).then_inc(diag_set, 1)
                    if hook:
                        hook()
                    if g > 0:
                        k = 2 * i + u
                        ls = ((g - 1) * 4 + blk) * 8 + k
                        if phase == 1:
                            kb = ((g - 1) * 2 + img) * 8 + k
                            own_wait(pool, g_ready, 8 * kb + 1)
                            pool.tensor_copy(selk[:, u, :], sel[:, bass.ds(k, 1), :].rearrange("p a m -> p (a m)")
                                             ).then_inc(selk_set, 1)
                    if g < PAIRS:
                        own_wait(pool, sums_in, n + 1 + 1)
                        pool.tensor_scalar(bnd[:, 2:6], ex[:, u, :], 1e-37, 1.01, ALU.add, ALU.mult).then_inc(bnd_step, 1)
                        own_wait(pool, bnd_step, 3 * n + 1)
                        pool.tensor_tensor(bnd[:, 0:2], bnd[:, 2:4], bnd[:, 4:6], ALU.mult).then_inc(bnd_step, 1)
                        own_wait(pool, bnd_step, 3 * n + 2)
                        pool.tensor_scalar(bnd[:, 6:7], bnd[:, 0:1], bnd[:, 1:2], None, ALU.max).then_inc(bnd_step, 1)
                        own_wait(pool, counted, n + 1)
                        pool.partition_all_reduce(cntm[:, :], cntp[:, u:u + 1], P, RMAX).then_inc(cnt_step, 1)
                        own_wait(pool, cnt_step, 2 * n + 1)
                        pool.tensor_copy(cnt[:, u:u + 1], cntm[0:1, :]).then_inc(cnt_step, 1)
                    if g > 0 and phase == 0:
                        ka = ((g - 1) * 2 + img) * 8 + k
                        own_wait(pool, y_out, 8 * ls + 8 + 1)
                        pool.tensor_copy(atab[:, bass.ds(k, 1), :].rearrange("p a k -> p (a k)"), yacc[:, u, :]
                                         ).then_inc(a_kept, 1)
                loop(pool, 8, body, keys if g > 0 and phase == 0 else None)

        @block.scalar
        def _(act):
            A = nc.scalar.activation
            for s in range(2):
                act.sem_inc(cur_free[s], 1)
                act.sem_inc(acc_free[s], 1)
            for s in range(2):
                act.sem_inc(pre_free[s], 1)
            act_in = 0

            def small_fn(out_, in_, fn, **kw):
                nonlocal act_in
                act_in += 1
                act.wait_ge(to_act, act_in)
                A(out_, in_, fn, **kw).then_inc(act_small, 1)

            act.wait_ge(pe_small, 1)
            A(kk[:, :], small[:, 0:TAPS], ACT.Exp, scale=-E_EXP).then_inc(act_small, 1)

            def stat_tile(n, c, u, buf, landed, loads, freed):
                act.wait_ge(landed, 16 * loads)
                A(buf[:, :], buf[:, :], ACT.Identity, scale=-1.0 / BLK, accum_out=pacc[:, u, 1:2]
                  ).then_inc(ps_step, 1)
                act.wait_ge(ps_step, 3 * n + 1)
                A(buf[:, :], buf[:, :], ACT.Square, scale=-float(BLK), bias=pacc[:, u, 1:2],
                  accum_out=pacc[:, u, 2:3]).then_inc(ps_step, 1)
                own_wait(act, ps_step, 3 * n + 2)
                act.sem_inc(freed, 1)
                for f in range(2):
                    last = A(px[f][:, bass.ds(c, 1)], pacc[:, u, f + 1:f + 2], ACT.Identity)
                last.then_inc(ps_step, 1)

            loop(act, C, lambda i, u: stat_tile(2 * i + u, 2 * i + u, u, pre[u], pre_in[u], i + 1, pre_free[u]))
            act.wait_ge(ps_step, 3 * C)
            act.sem_inc(pst_free, 1)
            act.wait_ge(filled, 4)
            act_in += 1
            act.wait_ge(to_act, act_in)
            A(krow_o[:, TAPS:2 * TAPS], krow_o[:, TAPS:2 * TAPS], ACT.Exp, scale=BETA,
              bias=col[0:32, C_EK:C_EK + 1]).then_inc(tabs_small, 1)
            small_fn(cc(W_NORM), cc(W_NORM), ACT.Sqrt)
            for g, blk in schedule():
                img, phase = divmod(blk, 2)
                def pair_std():
                    nonlocal act_in
                    small_fn(st[:, 5, :], st[:, 4, :], ACT.Sqrt)
                    act_in += 1
                    act.wait_ge(to_act, act_in)

                if g == 0 and blk == 0:
                    pair_std()

                def prepare(blk=blk, phase=phase):
                    nonlocal act_in
                    if blk == 0:
                        small_fn(st[:, 5, :], st[:, 4, :], ACT.Sqrt)
                    if phase == 1:
                        small_fn(cc(GATE), cc(REL), ACT.Tanh, scale=0.5)
                    act_in += 1
                    act.wait_ge(to_act, act_in)

                def body(i, u, hook=None, late=None, g=g, blk=blk, img=img, phase=phase):
                    i2 = 4 * blk + i
                    n = g * C + 2 * i2 + u
                    c = 2 * i2 + u
                    k = 2 * i + u
                    ls = ((g - 1) * 4 + blk) * 8 + k

                    def exp_sum(j, src, scale, bias, col_):
                        act.wait_ge(junk_w, 6 * n + j + 1)
                        ins = A(junk[:, 0:src.shape[1]], src, ACT.Exp, scale=cur[:, u, scale:scale + 1],
                                bias=cur[:, u, bias:bias + 1], accum_out=ex[:, u, col_:col_ + 1])
                        ins.then_inc(junk_w, 1)
                        return ins

                    def y_evac(e):
                        s = e // NCH
                        yb = y_bank(g, e)[0]
                        act.wait_ge(y_ready, 8 * ls + e + 1)
                        if phase == 0:
                            A(yb[:, :], yb[:, :], ACT.Square, bias=cc(BIASV),
                              accum_out=yacc[:, u, e:e + 1]).then_inc(y_out, 1)
                        else:
                            A(at[s][:, e % NCH * CH:(e % NCH + 1) * CH], yb[:, :], ACT.Identity,
                              bias=cc(BIASO)).then_inc(y_out, 1)

                    if g < PAIRS:
                        act.wait_ge(cur_set, n + 1)
                        act.wait_ge(x_in[u], LOADS * (g * (C // 2) + i2 + 1))
                        for s in range(2):
                            exp_sum(s, xt[u][:, s * TR // 2 * HC:(s * TR // 2 + TR // 2 + 2 * R) * HC], 3, 4, s)

                    def min_sums():
                        act.wait_ge(tap_done, TAPS * n + FIRST + 1)
                        exp_sum(2, accf[:, 0:BLK // 2], 5, 6, 2)
                        exp_sum(3, accf[:, BLK // 2:BLK], 5, 6, 3)
                        act.wait_ge(junk_w, 6 * n + 4 + 1)
                        act.sem_inc(sums_in, 1)

                    if hook:
                        hook()
                    if g == 0:
                        min_sums()
                    if g > 0 and phase == 1:
                        for e in range(NCH):
                            if g < PAIRS and e == EARLY:
                                min_sums()
                            y_evac(e)
                        act.wait_ge(y_out, 8 * ls + NCH + 1)
                        act.sem_inc(at_free[0], 1)
                        act.dma_start(tile_of(out, 2 * (g - 1) + img, 2 * k + 0), at[0][:, :]
                                      ).then_inc(out_st[0], 16)
                    if g > 0 and phase == 1:
                        for e in range(NCH, 2 * NCH):
                            y_evac(e)
                        act.wait_ge(y_out, 8 * ls + 2 * NCH + 1)
                        act.sem_inc(at_free[1], 1)
                        act.dma_start(tile_of(out, 2 * (g - 1) + img, 2 * k + 1), at[1][:, :]
                                      ).then_inc(out_st[1], 16)
                    if g > 0 and phase == 0:
                        ka = ((g - 1) * 2 + img) * 8 + k
                        act.wait_ge(a_kept, ka + 1)
                        for s in range(2):
                            if g < PAIRS and s == 1:
                                min_sums()
                            act.wait_ge(z_ready, 2 * ka + s + 1)
                            A(gates[:, bass.ds((2 * k + s) * MT, MT)], ps_t[:, 0:MT], ACT.Tanh, scale=0.5,
                              bias=cc(BIASZ)).then_inc(z_out, 1)
                            for e in range(NCH * s, NCH * s + NCH):
                                y_evac(e)
                            act.wait_ge(y_out, 8 * ls + 4 * s + 4 + 1)
                            act.sem_inc(at_free[s], 1)
                    if g < PAIRS - 1:
                        stat_tile(n + C, c, u, pst, pst_in, n + 1, pst_free)
                    if late:
                        late()
                    if g < PAIRS:
                        for e in range(NCH):
                            act.wait_ge(mix_ready, 4 * n + e + 1)
                            A(acc[u][:, e * CH:(e + 1) * CH], ps_mix[:, :], ACT.Identity, bias=cur[:, u, 2:3],
                              accum_out=xacc[:, u, e:e + 1]).then_inc(mix_out, 1)
                        act.wait_ge(mix_out, 4 * n + 4 + 1)
                        act.sem_inc(cur_free[u], 1)
                        dst = x1_d.rearrange("b c h w -> c b h w")[bass.ds(c, 1), 2 * g:2 * g + 2, :, :]
                        for q in range(QUARTERS):
                            for m in range(2):
                                act.dma_start(dst[0, m, :, q * TC:(q + 1) * TC].rearrange("(b r) c -> b r c", r=TR),
                                              acc[u][32 * q + m:32 * q + 32:2, :].rearrange("p (r c) -> p r c", c=TC)
                                              ).then_inc(x1_st[u], 16)
                        A(xacc[:, u, 0:4], xacc[:, u, 0:4],
                          ACT.Identity, scale=-1.0 / BLK, accum_out=xacc[:, u, 5:6]).then_inc(xs_step, 1)
                        act.wait_ge(xs_step, 4 * n + 1 + 1)
                        for j in range(2):
                            act.wait_ge(junk_w, 6 * n + 4 + j + 1)
                            A(junk[:, 0:BLK // 2], acc[u][:, j * BLK // 2:(j + 1) * BLK // 2], ACT.Square,
                              bias=xacc[:, u, 5:6], accum_out=xacc[:, u, j:j + 1]).then_inc(junk_w, 1)
                        act.wait_ge(junk_w, 6 * n + 6 + 1)
                        A(xacc[:, u, 0:2], xacc[:, u, 0:2], ACT.Identity, accum_out=xacc[:, u, 7:8]
                          ).then_inc(xs_step, 1)
                        own_wait(act, xs_step, 4 * n + 2 + 1)
                        for f in range(2):
                            A(p1[f][:, bass.ds(c, 1)], xacc[:, u, 5 + 2 * f:6 + 2 * f], ACT.Identity
                              ).then_inc(xs_step, 1)
                        own_wait(act, csum_ready, n + 1 + 1)
                        A(csum[:, bass.ds(c, 1), :].rearrange("p a k -> p (a k)"), ps_col[:, 0:2], ACT.Identity
                          ).then_inc(csum_out, 1)
                        act.sem_inc(acc_free[u], 1)
                loop(act, 8, body, prepare if g > 0 else None, pair_std if g < PAIRS - 1 and blk == 3 else None)
            for s in range(2):
                act.wait_ge(out_st[s], 16 * 8 * B + 1)

        @block.tensor
        def _(pe):
            M = nc.tensor.matmul
            for s in range(2):
                pe.sem_inc(x_free[s], 1)
            ins = 0

            def wait_operands():
                nonlocal ins
                ins += 1
                pe.wait_ge(to_pe, ins)

            def rep(a):
                return a.unsqueeze(1).to_broadcast([a.shape[0], QUARTERS, 32])

            pe.wait_ge(const_in, 16 * CONSTS)
            pe.wait_ge(filled, 1)
            M(small[:, 0:TAPS], fpt[:, :], basis[:, :], start=True, stop=True).then_inc(pe_small, 1)
            wait_operands()
            M(small[0:32, 0:2 * TAPS], const("fold"), sums[:, :], start=True, stop=True).then_inc(pe_small, 1)
            for i in range(4):
                wait_operands()
                M(small[:, 0:P], wraw[:, i, :], rep(ident[0:32, 0:32]), start=True, stop=True
                  ).then_inc(pe_small, 1)
            wait_operands()
            M(small[:, 0:P], wckr[:, :], ones[0:1, :], start=True, stop=True).then_inc(pe_small, 1)
            wait_operands()
            M(small[:, 0:1], wck, ones[:, 0:1], start=True, stop=True)
            M(small[:, 1:2], wck, cc(WCOL), start=True, stop=True)
            M(small[0:32, 2:3], wraw[:, 4, 0:32], ones[0:32, 0:1], start=True, stop=True).then_inc(pe_small, 1)

            def stats():
                for _ in range(2):
                    wait_operands()
                    M(small[:, 0:C], const("same"), st[:, 0, :], start=True, stop=True).then_inc(pe_small, 1)

            for g, blk in schedule():
                img, phase = divmod(blk, 2)
                if g == 0 and blk == 0:
                    stats()

                def prepare(blk=blk, img=img, phase=phase):
                    if blk == 0:
                        stats()
                        wait_operands()
                        for f in range(4):
                            last = M(small[:, 2 * f:2 * f + 2], tb4[:, f, :, :].rearrange("p q c -> p (q c)"), ident[:, 0:2], start=True, stop=True)
                        for m in range(2):
                            last = M(small[0:32, 32 * m + 32:32 * m + 64], csum[:, :, m], const("fold"), start=True, stop=True)
                        last.then_inc(pe_small, 1)
                    if phase == 0:
                        wait_operands()
                        M(small[:, 0:1], wv[:, :], cols[:, 0, img:img + 1], start=True, stop=True)
                        M(small[:, 1:2], wsq, cc(RM), start=True, stop=True).then_inc(pe_small, 1)
                        wait_operands()
                        M(small[:, 0:BW], ones[0:32, :], pp[:, :], start=True, stop=True).then_inc(pe_small, 1)
                        pe.wait_ge(wj_set, 2 * (g - 1) + img + 1)
                    if phase == 1:
                        wait_operands()
                        M(small[:, 0:1], const("qfold"), cc(ASUM), start=True, stop=True).then_inc(pe_small, 1)
                        wait_operands()
                        M(small[:, 0:1], wckp, cc(ZC), start=True, stop=True).then_inc(pe_small, 1)
                        wait_operands()
                        M(small[:, 0:1], wcq, cc(UC), start=True, stop=True)
                        M(small[:, 1:2], wck, cols[:, 3, img:img + 1], start=True, stop=True).then_inc(pe_small, 1)
                        wait_operands()
                        M(small[:, 0:1], wa[:, :], cols[:, 0, img:img + 1], start=True, stop=True
                          ).then_inc(pe_small, 1)

                def body(i, u, hook=None, late=None, g=g, blk=blk, img=img, phase=phase):
                    i2 = 4 * blk + i
                    n = g * C + 2 * i2 + u
                    k = 2 * i + u
                    ls = ((g - 1) * 4 + blk) * 8 + k
                    if hook:
                        hook()
                    if g > 0 and phase == 0:
                        ka = ((g - 1) * 2 + img) * 8 + k
                        for s in range(2):
                            pe.wait_ge(z_out, 2 * ka + s + 1)
                            pe.wait_ge(at_in[s], 16 * (ls + 1))
                            runs = at[s][:, :].rearrange("p (m j) -> p j m", j=BW)
                            for j in range(BW):
                                last = M(ps_t[:, 0:MT], wj[:, j, :], runs[:, j, :], start=(j == 0), stop=(j == BW - 1))
                            last.then_inc(z_ready, 1)
                            for e in range(NCH * s, NCH * s + NCH):
                                yb, deep = y_bank(g, e)
                                pe.wait_ge(y_out, 8 * ls + e + 2 - deep)
                                for h in range(2):
                                    lo = e % NCH * CH + 512 * h
                                    last = M(yb[:, 512 * h:512 * h + 512], wv[:, :], at[s][:, lo:lo + 512],
                                             start=True, stop=True)
                                last.then_inc(y_ready, 1)
                    if g > 0 and phase == 1:
                        kb = ((g - 1) * 2 + img) * 8 + k

                        def spread(e):
                            q = e // 2
                            pe.wait_ge(gx_ready, 8 * kb + e + 1)
                            for h in range(2):
                                lo = e % 2 * CH + 512 * h
                                last = M(ps_g[:, 512 * h:512 * h + 512], selk[32 * q:32 * q + 32, u, :],
                                         gates[32 * q:32 * q + 32, lo:lo + 512], start=True, stop=True)
                            last.then_inc(g_ready, 1)

                        pe.wait_ge(selk_set, kb + 1)
                        spread(0)
                        for e in range(2 * NCH):
                            if e % NCH == 0:
                                pe.wait_ge(at_in[e // NCH], 16 * (ls + 1))
                            if e + 1 < 2 * NCH:
                                spread(e + 1)
                            yb, deep = y_bank(g, e)
                            pe.wait_ge(y_out, 8 * ls + e + 2 - deep)
                            pe.wait_ge(gx_ready, 8 * kb + e + 1 + 1)
                            for h in range(2):
                                lo = e % NCH * CH + 512 * h
                                yh = yb[:, 512 * h:512 * h + 512]
                                M(yh, wa[:, :], at[e // NCH][:, lo:lo + 512], start=True, stop=False)
                                last = M(yh, wb[:, :], gx[:, e % 2, 512 * h:512 * h + 512], start=False, stop=True)
                            last.then_inc(y_ready, 1)
                    if late:
                        late()
                    if g < PAIRS:
                        pe.wait_ge(diag_set, n + 1)
                        pe.wait_ge(tap_done, TAPS * (n + 1) + 1)
                        X = xt[u][:, 0:HR * HC].rearrange("p (r c) -> p r c", c=HC)
                        for e in range(NCH):
                            pe.wait_ge(mix_out, 4 * n + e + 1)
                            for h in range(2):
                                r0 = (e * CH + 512 * h) // TC
                                mh = ps_mix[:, 512 * h:512 * h + 512]
                                M(mh, ident, X[:, R + r0:R + r0 + 512 // TC, R:R + TC], start=True, stop=False)
                                last = M(mh, diag[:, u, :], acc[u][:, r0 * TC:r0 * TC + 512], start=False, stop=True)
                            last.then_inc(mix_ready, 1)
                        pe.wait_ge(mix_ready, 4 * n + 4)
                        pe.sem_inc(x_free[u], 1)
                        pe.wait_ge(csum_out, n + 1)
                        pe.wait_ge(mix_out, 4 * n + 4 + 1)
                        for r in range(TR):
                            last = M(ps_col[:, 0:2], acc[u][:, r * TC:(r + 1) * TC], const("img"),
                                     start=(r == 0), stop=(r == TR - 1))
                        last.then_inc(csum_ready, 1)
                loop(pe, 8, body, prepare if g > 0 else None, stats if g < PAIRS - 1 and blk == 3 else None)

        @block.vector
        def _(dve):
            V = nc.vector
            links = 0
            pe_n = 0
            act_n = 0

            def link(i):
                nonlocal links
                links += 1
                i.then_inc(dve_small, 1)
                dve.wait_ge(dve_small, links)

            def from_pe():
                nonlocal pe_n
                pe_n += 1
                dve.wait_ge(pe_small, pe_n)

            def from_act():
                nonlocal act_n
                act_n += 1
                dve.wait_ge(act_small, act_n)

            def ts(out_, in_, s1, s2, o0, o1=None):
                if o1 is None:
                    link(V.tensor_scalar(out_, in_, s1, None, o0))
                else:
                    link(V.tensor_scalar(out_, in_, s1, s2, o0, o1))

            def tt(out_, a, b, op):
                link(V.tensor_tensor(out_, a, b, op))

            def stt(out_, a, s, b, o0, o1):
                link(V.scalar_tensor_tensor(out_, a, s, b, o0, o1))

            dve.wait_ge(const_in, 16 * CONSTS)
            from_act()
            tt(kk[:, :], kk[:, :], const("radial"), ALU.mult)
            ts(kk[:, :], kk[:, :], -NEG, None, ALU.min)
            for q in range(QUARTERS):
                link(V.tensor_copy(kq[32 * q:32 * q + 32, :], kk[32 * q:32 * q + 32, q * QB:(q + 1) * QB]))
            big = [at[0][:, 0:QB * TAPS].rearrange("p (t v) -> p t v", t=QB),
                   at[1][:, 0:QB * TAPS].rearrange("p (t v) -> p t v", t=QB)]
            tie = accf[:, 0:QB * TAPS].rearrange("p (t v) -> p t v", t=QB)
            every = kk[:, :].unsqueeze(1).to_broadcast([P, QB, TAPS])
            own = kq[:, :].unsqueeze(2).to_broadcast([P, QB, TAPS])
            dve.wait_ge(tie_in, 16)
            tt(big[0], every, own, ALU.is_equal)
            tt(big[0], big[0], tie, ALU.mult)
            tt(big[1], every, own, ALU.is_lt)
            tt(big[0], big[0], big[1], ALU.add)
            link(V.tensor_reduce(rank[:, :], big[0], AX_X, ALU.add))
            hot = [at[0][:, 0:QB * TAPS].rearrange("p (v t) -> p v t", t=QB),
                   at[1][:, 0:QB * TAPS].rearrange("p (v t) -> p v t", t=QB)]
            tt(hot[0], const("iota").unsqueeze(2).to_broadcast([P, TAPS, QB]),
               rank[:, :].unsqueeze(1).to_broadcast([P, TAPS, QB]), ALU.is_equal)
            tt(hot[1], hot[0], kq[:, :].unsqueeze(1).to_broadcast([P, TAPS, QB]), ALU.mult)
            link(V.tensor_reduce(sums[:, 0:TAPS], hot[1], AX_X, ALU.add))
            tt(hot[1], hot[0], const("offq").unsqueeze(1).to_broadcast([P, TAPS, QB]), ALU.mult)
            link(V.tensor_reduce(sums[:, TAPS:2 * TAPS], hot[1], AX_X, ALU.add))
            for s in range(2):
                dve.sem_inc(at_free[s], 1)
            dve.sem_inc(to_pe, 1)
            from_pe()
            from_pe()
            link(V.tensor_copy(krow_o[:, 0:TAPS], small[0:32, 0:TAPS]))
            ts(krow_o[:, TAPS:2 * TAPS], small[0:32, 0:TAPS], KCAP, None, ALU.min)
            dve.sem_inc(to_act, 1)
            link(V.tensor_copy(orow_o[:, :], small[0:32, TAPS:2 * TAPS]))
            dve.sem_inc(tabs_small, 1)
            for w in (wsq, wcq, wf1, wf2):
                dve.sem_inc(to_pe, 1)
                from_pe()
                tt(w, small[:, 0:P], const("bd"), ALU.mult)
            dve.sem_inc(to_pe, 1)
            from_pe()
            link(V.tensor_copy(cc(WCOL), small[:, 0:1]))
            tt(wck, small[:, 0:P], const("bd"), ALU.mult)
            dve.sem_inc(to_pe, 1)
            from_pe()
            link(V.tensor_copy(cc(W_SUM), small[:, 0:1]))
            ts(cc(W_NORM), small[:, 1:2], 1e-30, None, ALU.add)
            link(V.tensor_copy(col[0:32, WS_SUM:WS_SUM + 1], small[0:32, 2:3]))
            dve.sem_inc(to_act, 1)
            from_act()
            ts(cc(TMP), cc(W_SUM), 0.0, 2.0, ALU.is_ge, ALU.mult)
            ts(cc(TMP), cc(TMP), -1.0, None, ALU.add)
            link(V.reciprocal(cc(W_INV), cc(W_NORM)))
            tt(cc(W_ALPHA), cc(W_INV), cc(TMP), ALU.mult)
            tt(cc(W_IALPHA), cc(W_NORM), cc(TMP), ALU.mult)
            ts(wckp, wck, cc(W_ALPHA), None, ALU.mult)
            tt(ipw, wckp, ident, ALU.add)
            tt(cc(TMP), cc(W_ALPHA), cc(W_SUM), ALU.mult)
            ts(cc(TMP), cc(TMP), 0.5, 1.0, ALU.mult, ALU.add)
            link(V.reciprocal(cc(W_IDEN), cc(TMP)))

            def stats(nmean, sq):
                ts(st[:, 0, :], nmean[:, :], -float(BLK), None, ALU.mult)
                dve.sem_inc(to_pe, 1)
                from_pe()
                link(V.tensor_copy(st[:, 2, :], small[:, 0:C]))

                def grouped(out_, in_, scale, bias):
                    pair = in_.rearrange("p (g a) -> p g a", a=2)
                    tt(st[:, 5, 0:GC], pair[:, :, 0], pair[:, :, 1], ALU.add)
                    ts(out_.rearrange("p (g a) -> p g a", a=2), st[:, 5, 0:GC].unsqueeze(2).to_broadcast([P, GC, 2]),
                       scale, bias, ALU.mult, ALU.add)

                grouped(st[:, 1, :], st[:, 2, :], 0.5 / HW, 0.0)
                stt(st[:, 3, :], nmean[:, :], 1.0, st[:, 1, :], ALU.mult, ALU.add)
                stt(st[:, 4, :], st[:, 3, :], float(BLK), st[:, 3, :], ALU.mult, ALU.mult)
                tt(st[:, 0, :], st[:, 4, :], sq[:, :], ALU.add)
                dve.sem_inc(to_pe, 1)
                from_pe()
                link(V.tensor_copy(st[:, 7, :], small[:, 0:C]))
                grouped(st[:, 4, :], st[:, 7, :], 0.5 / HW, EPS)
                dve.sem_inc(to_act, 1)
                from_act()
                link(V.reciprocal(st[:, 6, :], st[:, 5, :]))
                tt(st[:, 6, :], st[:, 6, :], st[:, 4, :], ALU.mult)
                tt(st[:, 3, :], st[:, 6, :], st[:, 5, :], ALU.add)
                ts(st[:, 3, :], st[:, 3, :], 0.5, None, ALU.mult)
                link(V.reciprocal(st[:, 6, :], st[:, 3, :]))

            def prepare_pair():
                stats(px[0], px[1])
                link(V.tensor_copy(stat[:, :, 0], st[:, 3, :]))
                link(V.tensor_copy(stat[:, :, 1], st[:, 6, :]))
                stt(stat[:, :, 2], st[:, 1, :], -1.0, st[:, 6, :], ALU.mult, ALU.mult)
                ts(stat[:, :, 3], st[:, 6, :], BETA, None, ALU.mult)
                ts(stat[:, :, 4], stat[:, :, 2], BETA, -OFFS, ALU.mult, ALU.add)
                ts(stat[:, :, 5], st[:, 6, :], -BETA, None, ALU.mult)
                ts(stat[:, :, 6], stat[:, :, 2], -BETA, -OFFS, ALU.mult, ALU.add)
                ts(stat[:, :, 7], st[:, 6, :], 0.0, None, ALU.mult)
                dve.sem_inc(to_pool, 1)
                dve.sem_inc(to_act, 1)

            def prepare_attention():
                stats(p1[0], p1[1])
                link(V.tensor_copy(tb[:, 0, :], st[:, 1, :]))
                link(V.tensor_copy(tb[:, 1, :], st[:, 6, :]))
                stt(st[:, 4, :], st[:, 1, :], -float(HW), st[:, 2, :], ALU.mult, ALU.add)
                tt(tb[:, 3, :], st[:, 4, :], st[:, 6, :], ALU.mult)
                tt(st[:, 4, :], st[:, 7, :], st[:, 6, :], ALU.mult)
                tt(tb[:, 2, :], st[:, 4, :], st[:, 6, :], ALU.mult)
                for q in range(QUARTERS):
                    link(V.tensor_copy(tb4[:, :, q, :], tb[:, :, :]))
                dve.sem_inc(to_pe, 1)
                from_pe()
                link(V.tensor_copy(cols[:, :, :].rearrange("p a b -> p (a b)"), small[:, 0:8]))
                link(V.tensor_copy(classes[:, :, :].rearrange("p a b -> p (a b)"), small[0:32, 32:96]))

            def prepare_gates(img):
                m, r = cols[:, 0, img:img + 1], cols[:, 1, img:img + 1]
                ts(wv[:, :], ipw, r, None, ALU.mult)
                tt(cc(RM), r, m, ALU.mult)
                dve.sem_inc(to_pe, 1)
                from_pe()
                ts(cc(BIASV), small[:, 0:1], -1.0, None, ALU.mult)
                tt(cc(BIASZ), bcol[:, 0:1], small[:, 1:2], ALU.subtract)
                ts(cc(TMP), m, float(HW // BW), None, ALU.mult)
                tt(cc(WRC)[0:32], cc(WS_SUM)[0:32], r[0:32], ALU.mult)
                ts(pp[:, :], classes[:, img, :], cc(TMP)[0:32], cc(WRC)[0:32], ALU.subtract, ALU.mult)
                ts(cc(TMP)[0:32], bcol[0:32, 4:5], float(HW // BW), None, ALU.mult)
                ts(pp[:, :], pp[:, :], cc(TMP)[0:32], None, ALU.add)
                dve.sem_inc(to_pe, 1)
                from_pe()
                ts(skb[:, :], small[:, 0:BW], 1.0 / HW, None, ALU.mult)
                link(V.tensor_reduce(cc(SKSUM), skb[:, :], AX_X, ALU.add))
                ts(skr[:, :], skb[:, :], r, None, ALU.mult)
                dve.sem_inc(to_pool, 1)
                ts(cc(BIASZ), cc(BIASZ), cc(SKSUM), 0.5, ALU.mult, ALU.mult)
                dve.sem_inc(to_act, 1)

            def prepare_output(g, img):
                m, r = cols[:, 0, img:img + 1], cols[:, 1, img:img + 1]
                b2, sh = cols[:, 2, img:img + 1], cols[:, 3, img:img + 1]
                dve.wait_ge(a_kept, 8 * (2 * (g - 1) + img + 1) + 1)
                dve.wait_ge(y_out, 8 * (8 * (4 * (g - 1) + 2 * img + 1)) + 1)
                link(V.tensor_reduce(cc(ASUM), atab[:, :, :].rearrange("p a b -> p (a b)"), AX_X, ALU.add))
                dve.sem_inc(to_pe, 1)
                from_pe()
                tt(cc(ZC), small[:, 0:1], b2, ALU.subtract)
                ts(cc(ZC), cc(ZC), 0.5, None, ALU.mult)
                dve.sem_inc(to_pe, 1)
                from_pe()
                tt(cc(KP), small[:, 0:1], cc(W_IDEN), ALU.mult)
                stt(cc(UC), cc(KP), -0.5, cc(ZC), ALU.mult, ALU.add)
                tt(cc(UC), cc(UC), cc(W_IALPHA), ALU.mult)
                stt(cc(UC), sh, bcol[:, 3:4], cc(UC), ALU.mult, ALU.add)
                dve.sem_inc(to_pe, 1)
                from_pe()
                stt(cc(TMP), bcol[:, 3:4], float(HW), small[:, 1:2], ALU.mult, ALU.add)
                tt(cc(TMP), cc(TMP), bcol[:, 1:2], ALU.mult)
                tt(cc(REL), small[:, 0:1], cc(TMP), ALU.add)
                dve.sem_inc(to_act, 1)
                from_act()
                ts(cc(GATE), cc(GATE), -0.5, 0.5, ALU.mult, ALU.add)
                tt(cc(RG), cc(GATE), r, ALU.mult)
                ts(cc(R5), r, 0.5, None, ALU.mult)
                ts(wtmp, wf2, cc(R5), None, ALU.mult)
                stt(wa[:, :], wf1, cc(RG), wtmp, ALU.mult, ALU.add)
                tt(wa[:, :], wa[:, :], ident, ALU.add)
                ts(wb[:, :], wtmp, -1.0, None, ALU.mult)
                dve.sem_inc(to_pe, 1)
                from_pe()
                tt(cc(TMP), bcol[:, 2:3], m, ALU.add)
                tt(cc(BIASO), cc(TMP), small[:, 0:1], ALU.subtract)
                dve.sem_inc(to_act, 1)

            for g, blk in schedule():
                img, phase = divmod(blk, 2)
                if g == 0 and blk == 0:
                    dve.wait_ge(ps_step, 3 * C)
                    prepare_pair()

                def next_pair(g=g):
                    dve.wait_ge(ps_step, 3 * (g + 2) * C)
                    prepare_pair()

                def prepare(g=g, blk=blk, img=img, phase=phase):
                    if blk == 0:
                        dve.wait_ge(xs_step, 4 * g * C + 1)
                        dve.wait_ge(csum_out, g * C + 1)
                        prepare_attention()
                    if phase == 0:
                        prepare_gates(img)
                    else:
                        prepare_output(g, img)

                def body(i, u, hook=None, late=None, g=g, blk=blk, img=img, phase=phase):
                    i2 = 4 * blk + i
                    n = g * C + 2 * i2 + u
                    k = 2 * i + u
                    ls = ((g - 1) * 4 + blk) * 8 + k
                    kb = ((g - 1) * 2 + img) * 8 + k

                    def gate_chunk(e):
                        if e % NCH == 0:
                            dve.wait_ge(at_in[e // NCH], 16 * (ls + 1))
                        if e >= 2:
                            dve.wait_ge(y_ready, 8 * ls + e - 1)
                        dve.wait_ge(g_ready, 8 * kb + e + 1 + 1)
                        V.scalar_tensor_tensor(gx[:, e % 2, :], at[e // NCH][:, e % NCH * CH:(e % NCH + 1) * CH],
                                               cols[:, 0, img:img + 1], ps_g[:, :], ALU.subtract, ALU.mult
                                               ).then_inc(gx_ready, 1)

                    if g == PAIRS:
                        if hook:
                            hook()
                        if phase == 1:
                            for e in range(2 * NCH):
                                gate_chunk(e)
                        return

                    def shifted(off):
                        return xt[u][:, bass.ds(off, TR * HC)].rearrange("p (r c) -> p r c", c=HC)[:, :, 0:TC]

                    def block_of(a):
                        return a[:, :].rearrange("p (r c) -> p r c", c=TC)

                    def offsets(t0, count):
                        return nc.values_load_multi_w_load_instructions(
                            orow[0:1, u, bass.ds(t0, count)], engines=[mybir.EngineType.DVE], min_val=0,
                            max_val=2 * R * HC + 2 * R,
                            skip_runtime_bounds_check_because="a permutation of the table of offsets")[1]

                    dve.wait_ge(row_in[u], 32 * (g * (C // 2) + i2 + 1))
                    dve.wait_ge(cur_set, n + 1)
                    V.tensor_scalar(pen[:, u, :], krow[:, u, 0:TAPS], cur[:, u, 0:1], None, ALU.mult
                                    ).then_inc(pen_set, 1)
                    off = offsets(0, FIXED // 4)
                    dve.wait_ge(x_in[u], LOADS * (g * (C // 2) + i2 + 1))
                    dve.wait_ge(sums_in, n + 1)
                    for t in range(FIXED):
                        if t == FIRST:
                            dve.wait_ge(x1_st[u], STORES * (g * (C // 2) + i2) + 1)
                            dve.wait_ge(acc_free[u], g * (C // 2) + i2 + 1)
                        if t in (1, 5, 9):
                            off += offsets(len(off), FIXED // 4)
                        in1 = shifted(CENTRE) if t == 0 else block_of(accf if t <= FIRST else acc[u])
                        if t == 0:
                            dve.wait_ge(pen_set, n + 1)
                        dve.wait_ge(tap_done, TAPS * n + t + 1)
                        V.scalar_tensor_tensor(block_of(accf if t < FIRST else acc[u]), shifted(off[t]),
                                               pen[:, u, t:t + 1], in1, ALU.subtract, ALU.max).then_inc(tap_done, 1)
                        if hook and t == HOOK_AT:
                            hook()
                        if g > 0 and phase == 1 and t in GATE_AT:
                            gate_chunk(GATE_AT.index(t))
                        if late and t == FIXED - 1:
                            late()
                        if t == COUNT_AT:
                            dve.wait_ge(bnd_step, 3 * n + 3)
                            V.tensor_scalar(flag[:, :], krow[:, u, TAPS:2 * TAPS], bnd[:, 6:7], 0.0, ALU.is_lt, ALU.add,
                                            accum_out=cntp[:, u:u + 1]).then_inc(counted, 1)
                    own_wait(dve, cnt_step, 2 * n + 2)
                    need = dve.value_load(cnt[0:1, u:u + 1], min_val=0, max_val=TAPS)

                    def tap_groups(lo, hi):
                        with dve.Fori(lo, hi) as grp:
                            t0 = FIXED + grp * GRP
                            with dve.If(t0 < need):
                                off = offsets(t0, GRP)

                                def taps_from(j):
                                    dve.wait_ge(tap_done, TAPS * n + t0 + j + 1)
                                    V.scalar_tensor_tensor(
                                        block_of(acc[u]), shifted(off[j]), pen[:, u, bass.ds(t0 + j, 1)],
                                        block_of(acc[u]), ALU.subtract, ALU.max).then_inc(tap_done, 1)
                                    if j + 1 < GRP:
                                        with dve.If(t0 + j + 1 < need):
                                            taps_from(j + 1)
                                        with dve.Else():
                                            dve.sem_inc(tap_done, GRP - j - 1)

                                taps_from(0)
                            with dve.Else():
                                dve.sem_inc(tap_done, GRP)

                    tap_groups(0, NEAR)
                    with dve.If(FIXED + NEAR * GRP < need):
                        tap_groups(NEAR, GROUPS)
                    with dve.Else():
                        dve.sem_inc(tap_done, (GROUPS - NEAR) * GRP)
                loop(dve, 8, body, prepare if g > 0 else None, next_pair if g < PAIRS - 1 and blk == 3 else None)


_INS = ["x", "L0_conv_finsler_params", "L1_conv_w_ck", "L1_conv_b_ck", "L1_conv_w_cq", "L1_conv_b_cq", "L1_conv_w_sk",
        "L1_conv_b_sk", "L1_conv_w_sq", "L1_conv_b_sq", "L1_conv_w_f", "L1_conv_b_f"]


def kernel(**inputs):
    import concourse.bacc as _bacc
    from concourse.bass_utils import run_bass_kernel_spmd as _run

    nc = _bacc.Bacc("TRN2", target_bir_lowering=False, num_devices=1)
    arrays, args = {}, []
    named = [(n, np.ascontiguousarray(inputs[n])) for n in _INS] + list(shape_constants().items())
    for name, a in named:
        arrays[f"in_{name}"] = a
        args.append(nc.dram_tensor(f"in_{name}", a.shape, mybir.dt.from_np(a.dtype), kind="ExternalInput").ap())
    args.append(nc.dram_tensor("out_0", (B, C, H, W), F32, kind="ExternalOutput").ap())
    build(nc, *args)
    r = _run(nc, [arrays], core_ids=[0])
    return r.results[0]["out_0"]
```
